# Optimizing a Trainium2 kernel written in Bass

```python
import numpy as np
import jax
import jax.numpy as jnp

def _softmax(x, axis=-1):
    return jax.nn.softmax(x, axis=axis)

def _gelu(x):
    return jax.nn.gelu(x, approximate=True)

def _silu(x):
    return jax.nn.silu(x)

def _sigmoid(x):
    return jax.nn.sigmoid(x)

def _layernorm(x, axis=-1, eps=1e-05):
    m = jnp.mean(x, axis=axis, keepdims=True)
    v = jnp.var(x, axis=axis, keepdims=True)
    return (x - m) / jnp.sqrt(v + eps)

def _scatter_add(tgt, idx, src, axis=0):
    return tgt.at[idx].add(src)

def _segment_sum(src, seg, n):
    return jax.ops.segment_sum(src, seg, n)
kernel_name = 'mk_gnn_preln_d4_gnn_r8_c9e156'

def setup_inputs(seed: int=0):
    np.random.seed(seed)
    _w = jnp.asarray

    def _rec_inputs():
        import jax
        import jax.numpy as jnp
        _gk = jax.random.key(seed)
        x = -0.000202 + 1 * jax.random.normal(jax.random.fold_in(_gk, 1), (6250, 64), jnp.float32)
        _s = jax.random.randint(jax.random.fold_in(_gk, 2), (100000,), 0, 6250, jnp.int32)
        _d = jax.random.randint(jax.random.fold_in(_gk, 3), (100000,), 0, 6250, jnp.int32)
        _loop = jnp.arange(6250, dtype=jnp.int32)
        src = jnp.concatenate([_s, _d, _loop])
        dst = jnp.concatenate([_d, _s, _loop])
        _o = jnp.argsort(dst, stable=True)
        src = src[_o]
        dst = dst[_o]
        edge_attr_8 = 0.000254156 + 0.999948 * jax.random.normal(jax.random.fold_in(_gk, 12), (206250, 8), jnp.float32)
        edge_type_16 = jax.random.randint(jax.random.fold_in(_gk, 14), (206250,), 0, 16, jnp.int32)
        edge_weight = jax.random.uniform(jax.random.fold_in(_gk, 15), (206250,), jnp.float32, 0.0, 1)
        return (x, src, dst, edge_attr_8, edge_type_16, edge_weight)
    x, src, dst, edge_attr_8, edge_type_16, edge_weight = _rec_inputs()

    def _L0_gnn_setup():
        import jax, jax.numpy as jnp
        import numpy as np
        N_NODES = 12500
        N_EDGES = 156250
        IN_DIM = 64
        OUT_DIM = 64
        N_BASES = 16
        L2_EPS = 1e-12
        key = jax.random.key(seed)
        ks = jax.random.split(key, 7)
        return {'x': jax.random.normal(ks[0], (N_NODES, IN_DIM), dtype=jnp.float32), 'edge_index': jax.random.randint(ks[1], (2, N_EDGES), 0, N_NODES, dtype=jnp.int64) if jax.config.jax_enable_x64 else jax.random.randint(ks[1], (2, N_EDGES), 0, N_NODES, dtype=jnp.int32), 'basis_msg_wt': jax.random.normal(ks[2], (IN_DIM, OUT_DIM, N_BASES), dtype=jnp.float32) * 0.1, 'basis_msg_bias': jax.random.normal(ks[3], (OUT_DIM, N_BASES), dtype=jnp.float32) * 0.1, 'basis_self_wt': jax.random.normal(ks[4], (IN_DIM, OUT_DIM, N_BASES), dtype=jnp.float32) * 0.1, 'basis_self_bias': jax.random.normal(ks[5], (OUT_DIM, N_BASES), dtype=jnp.float32) * 0.1, 'lin_comb': jax.random.normal(ks[6], (1, N_BASES), dtype=jnp.float32) * 0.1}
    _L0_gnn_all = _L0_gnn_setup()
    _L0_gnn_in = {k: v for k, v in _L0_gnn_all.items() if k in ('basis_msg_wt', 'basis_msg_bias', 'basis_self_wt', 'basis_self_bias', 'lin_comb')}
    del _L0_gnn_all

    def _L1_gnn_setup():
        import jax, jax.numpy as jnp
        import numpy as np
        N_NODES = 12500
        N_EDGES = 125000
        D_IN = 64
        D_OUT = 64
        N_RELS = 16
        key = jax.random.key(seed)
        k1, k2, k3, k4, k5 = jax.random.split(key, 5)
        feat = jax.random.normal(k1, (N_NODES, D_IN), dtype=jnp.float32)
        weight = jax.random.normal(k2, (N_RELS, D_IN, D_OUT), dtype=jnp.float32) * 0.05
        src = jax.random.randint(k3, (N_EDGES,), 0, N_NODES)
        dst = jax.random.randint(k4, (N_EDGES,), 0, N_NODES)
        etypes = jax.random.randint(k5, (N_EDGES,), 0, N_RELS)
        return {'feat': feat, 'weight': weight, 'src': src, 'dst': dst, 'etypes': etypes}
    _L1_gnn_all = _L1_gnn_setup()
    _L1_gnn_in = {k: v for k, v in _L1_gnn_all.items() if k in ('weight',)}
    del _L1_gnn_all

    def _L2_gnn_setup():
        import jax, jax.numpy as jnp
        import numpy as np
        N_NODES = 12500
        N_EDGES = 150000
        N_DIM = 64

        def _spmm(edge_vals, edge_index, x):
            dst, src = (edge_index[0], edge_index[1])
            msgs = edge_vals[:, None] * x[src]
            return jax.ops.segment_sum(msgs, dst, num_segments=x.shape[0])
        key = jax.random.key(seed)
        k1, k2, k3 = jax.random.split(key, 3)
        all_emb = jax.random.normal(k1, (N_NODES, N_DIM), dtype=jnp.float32) * 0.1
        edge_vals = jax.random.uniform(k2, (N_EDGES,), dtype=jnp.float32)
        edge_index = jax.random.randint(k3, (2, N_EDGES), 0, N_NODES, dtype=jnp.int64)
        return {'all_emb': all_emb, 'edge_vals': edge_vals, 'edge_index': edge_index, 'n_layers': 3}
    _L2_gnn_all = _L2_gnn_setup()
    _L2_gnn_in = {k: v for k, v in _L2_gnn_all.items() if k in ()}
    del _L2_gnn_all

    def _L3_gnn_setup():
        import jax, jax.numpy as jnp
        import numpy as np
        N = 12500
        E = 200000
        IN = 64
        OUT = 64
        ED = 8
        H1 = OUT
        H2 = OUT // 2
        NEG_SLOPE = 0.01
        key = jax.random.key(seed)
        ks = jax.random.split(key, 16)
        s = 0.05
        x = jax.random.normal(ks[0], (N, IN), dtype=jnp.float32)
        edge_index = jax.random.randint(ks[1], (2, E), 0, N, dtype=jnp.int64)
        edge_attr = jax.random.normal(ks[2], (E, ED), dtype=jnp.float32)
        W_src = jax.random.normal(ks[3], (OUT, IN), dtype=jnp.float32) * s
        b_src = jnp.zeros((OUT,), jnp.float32)
        W_tgt = jax.random.normal(ks[4], (OUT, IN), dtype=jnp.float32) * s
        b_tgt = jnp.zeros((OUT,), jnp.float32)
        W_edge = jax.random.normal(ks[5], (OUT, ED), dtype=jnp.float32) * s
        b_edge = jnp.zeros((OUT,), jnp.float32)
        W1 = jax.random.normal(ks[6], (H1, 3 * OUT), dtype=jnp.float32) * s
        b1 = jnp.zeros((H1,), jnp.float32)
        W2 = jax.random.normal(ks[7], (H2, H1), dtype=jnp.float32) * s
        b2 = jnp.zeros((H2,), jnp.float32)
        W3 = jax.random.normal(ks[8], (1, H2), dtype=jnp.float32) * s
        b3 = jnp.zeros((1,), jnp.float32)
        return dict(x=x, edge_index=edge_index, edge_attr=edge_attr, W_src=W_src, b_src=b_src, W_tgt=W_tgt, b_tgt=b_tgt, W_edge=W_edge, b_edge=b_edge, W1=W1, b1=b1, W2=W2, b2=b2, W3=W3, b3=b3)
    _L3_gnn_all = _L3_gnn_setup()
    _L3_gnn_in = {k: v for k, v in _L3_gnn_all.items() if k in ('W_src', 'b_src', 'W_tgt', 'b_tgt', 'W_edge', 'b_edge', 'W1', 'b1', 'W2', 'b2', 'W3', 'b3')}
    del _L3_gnn_all
    return {'x': x, 'src': src, 'dst': dst, 'edge_attr_8': edge_attr_8, 'edge_type_16': edge_type_16, 'edge_weight': edge_weight, 'L0_gnn_basis_msg_wt': _L0_gnn_in['basis_msg_wt'], 'L0_gnn_basis_msg_bias': _L0_gnn_in['basis_msg_bias'], 'L0_gnn_basis_self_wt': _L0_gnn_in['basis_self_wt'], 'L0_gnn_basis_self_bias': _L0_gnn_in['basis_self_bias'], 'L0_gnn_lin_comb': _L0_gnn_in['lin_comb'], 'L1_gnn_weight': _L1_gnn_in['weight'], 'L3_gnn_W_src': _L3_gnn_in['W_src'], 'L3_gnn_b_src': _L3_gnn_in['b_src'], 'L3_gnn_W_tgt': _L3_gnn_in['W_tgt'], 'L3_gnn_b_tgt': _L3_gnn_in['b_tgt'], 'L3_gnn_W_edge': _L3_gnn_in['W_edge'], 'L3_gnn_b_edge': _L3_gnn_in['b_edge'], 'L3_gnn_W1': _L3_gnn_in['W1'], 'L3_gnn_b1': _L3_gnn_in['b1'], 'L3_gnn_W2': _L3_gnn_in['W2'], 'L3_gnn_b2': _L3_gnn_in['b2'], 'L3_gnn_W3': _L3_gnn_in['W3'], 'L3_gnn_b3': _L3_gnn_in['b3']}

def reference(x, src, dst, edge_attr_8, edge_type_16, edge_weight, L0_gnn_basis_msg_wt, L0_gnn_basis_msg_bias, L0_gnn_basis_self_wt, L0_gnn_basis_self_bias, L0_gnn_lin_comb, L1_gnn_weight, L3_gnn_W_src, L3_gnn_b_src, L3_gnn_W_tgt, L3_gnn_b_tgt, L3_gnn_W_edge, L3_gnn_b_edge, L3_gnn_W1, L3_gnn_b1, L3_gnn_W2, L3_gnn_b2, L3_gnn_W3, L3_gnn_b3):
    import jax
    import jax.numpy as jnp

    def _L0_gnn_ref(x, edge_index, basis_msg_wt, basis_msg_bias, basis_self_wt, basis_self_bias, lin_comb):
        import jax, jax.numpy as jnp
        import numpy as np
        N_NODES = 12500
        N_EDGES = 156250
        IN_DIM = 64
        OUT_DIM = 64
        N_BASES = 16
        L2_EPS = 1e-12
        c = lin_comb[0]
        W_msg = jnp.einsum('iob,b->io', basis_msg_wt, c)
        b_msg = basis_msg_bias @ c
        W_self = jnp.einsum('iob,b->io', basis_self_wt, c)
        b_self = basis_self_bias @ c
        src, dst = (edge_index[0], edge_index[1])
        msg = x[src] @ W_msg + b_msg
        agg = jax.ops.segment_sum(msg, dst, num_segments=x.shape[0])
        x_self = x @ W_self + b_self
        out = agg + x_self
        norm = jnp.linalg.norm(out, axis=-1, keepdims=True)
        return out / jnp.maximum(norm, L2_EPS)

    def _L1_gnn_ref(feat, weight, src, dst, etypes):
        import jax, jax.numpy as jnp
        import numpy as np
        N_NODES = 12500
        N_EDGES = 125000
        D_IN = 64
        D_OUT = 64
        N_RELS = 16
        h = feat[src]
        n_rels = weight.shape[0]
        e, d_out = (h.shape[0], weight.shape[2])

        def step(m, rw):
            r, w_r = rw
            mask = jnp.where(etypes == r, 1.0, 0.0).astype(h.dtype)
            m = m + mask[:, None] * (h @ w_r)
            return (m, None)
        m0 = jnp.zeros((e, d_out), dtype=h.dtype)
        m, _ = jax.lax.scan(step, m0, (jnp.arange(n_rels), weight))
        out = jax.ops.segment_sum(m, dst, num_segments=feat.shape[0])
        return out

    def _L2_gnn_ref(all_emb, edge_vals, edge_index, n_layers):
        import jax, jax.numpy as jnp
        import numpy as np
        N_NODES = 12500
        N_EDGES = 150000
        N_DIM = 64

        def _spmm(edge_vals, edge_index, x):
            dst, src = (edge_index[0], edge_index[1])
            msgs = edge_vals[:, None] * x[src]
            return jax.ops.segment_sum(msgs, dst, num_segments=x.shape[0])
        emb = all_emb
        acc = all_emb
        for _ in range(n_layers):
            emb = _spmm(edge_vals, edge_index, emb)
            acc = acc + emb
        return acc / jnp.float32(n_layers + 1)

    def _L3_gnn_ref(x, edge_index, edge_attr, W_src, b_src, W_tgt, b_tgt, W_edge, b_edge, W1, b1, W2, b2, W3, b3):
        import jax, jax.numpy as jnp
        import numpy as np
        N = 12500
        E = 200000
        IN = 64
        OUT = 64
        ED = 8
        H1 = OUT
        H2 = OUT // 2
        NEG_SLOPE = 0.01
        src, tgt = (edge_index[0], edge_index[1])
        x_source = x @ W_src.T + b_src
        x_target = x @ W_tgt.T + b_tgt
        edge_trans = edge_attr @ W_edge.T + b_edge
        combined = jnp.concatenate([x_source[src], x_target[tgt], edge_trans], axis=1)
        h = jax.nn.leaky_relu(combined @ W1.T + b1, NEG_SLOPE)
        h = jax.nn.leaky_relu(h @ W2.T + b2, NEG_SLOPE)
        e = (h @ W3.T + b3)[:, 0]
        e = jax.nn.relu(e)
        msg = e[:, None] * x_source[src]
        out = jax.ops.segment_sum(msg, tgt, num_segments=x.shape[0])
        return out + x_target
    edge_index = jnp.stack([src, dst])
    h = jnp.maximum(_layernorm(x, axis=-1), 0.0)
    x = x + _L0_gnn_ref(h, edge_index, L0_gnn_basis_msg_wt, L0_gnn_basis_msg_bias, L0_gnn_basis_self_wt, L0_gnn_basis_self_bias, L0_gnn_lin_comb)
    h = jnp.maximum(_layernorm(x, axis=-1), 0.0)
    x = x + _L1_gnn_ref(h, L1_gnn_weight, src, dst, edge_type_16)
    h = jnp.maximum(_layernorm(x, axis=-1), 0.0)
    x = x + _L2_gnn_ref(h, edge_weight, edge_index, 3)
    h = jnp.maximum(_layernorm(x, axis=-1), 0.0)
    x = x + _L3_gnn_ref(h, edge_index, edge_attr_8, L3_gnn_W_src, L3_gnn_b_src, L3_gnn_W_tgt, L3_gnn_b_tgt, L3_gnn_W_edge, L3_gnn_b_edge, L3_gnn_W1, L3_gnn_b1, L3_gnn_W2, L3_gnn_b2, L3_gnn_W3, L3_gnn_b3)
    return x

_drawn_inputs = setup_inputs


def setup_inputs(seed=0):
    import zlib

    import numpy as np

    out = dict(_drawn_inputs(seed))
    spreads = {'L3_gnn_b_src': (0.0, 0.8),
     'L3_gnn_b_tgt': (0.0, 0.8),
     'L3_gnn_b_edge': (0.0, 0.8),
     'L3_gnn_b1': (0.0, 2.0),
     'L3_gnn_b2': (0.0, 2.0)}
    factors = {'edge_attr_8': 8.0,
     'L0_gnn_basis_self_wt': 8.0,
     'L0_gnn_basis_self_bias': 45.719,
     'L3_gnn_W_src': 8.0,
     'L3_gnn_W_tgt': 8.0,
     'L3_gnn_W_edge': 8.0,
     'L3_gnn_W1': 8.0,
     'L3_gnn_W2': 8.0,
     'L3_gnn_W3': 8.0}
    for name, (base, spread) in spreads.items():
        noise = np.random.default_rng([zlib.crc32(name.encode()), seed]).standard_normal(out[name].shape)
        drawn = base * np.exp(spread * noise) if base else spread * noise
        out[name] = jnp.asarray(drawn.astype(out[name].dtype))
    for name, factor in factors.items():
        out[name] = (out[name] * factor).astype(out[name].dtype)
    return out
```

```python
from contextlib import ExitStack

import concourse.bass as bass
from concourse import mybir

F32 = mybir.dt.float32
I32 = mybir.dt.int32
ALU = mybir.AluOpType
ACT = mybir.ActivationFunctionType
AX = mybir.AxisListType

P = 128
LN_EPS = 1e-5
L2_EPS = 1e-12
NEG_SLOPE = 0.01
G = 8
R = 4


def gnn_kernel(nc, x, src, dst, edge_attr, etype, eweight, msg_wt, msg_b, self_wt, self_b, lin, rel_w,
               W_src, b_src, W_tgt, b_tgt, W_edge, b_edge, W1, b1, W2, b2, W3, b3, out):
    N, D = x.shape
    E = src.shape[0]
    EA = edge_attr.shape[1]
    NREL = rel_w.shape[0]
    NBASE = msg_wt.shape[2]
    H2 = W2.shape[0]
    NODE_BLOCKS = -(-N // P)
    BG = 4
    NJ = -(-NODE_BLOCKS // BG)
    NB = NJ * BG
    NP = NB * P
    TILES = -(-E // P)
    NC = -(-(TILES + NODE_BLOCKS - 1) // P)
    STEPS = NC * P
    assert STEPS % (G * R) == 0 and D == 64 and G * EA == 64 and H2 == 32
    NG = STEPS // G
    PAD_DST = NODE_BLOCKS * P - 1
    assert PAD_DST >= N
    DA = D + 1
    NH = 3
    NT = G
    ACC_ROWS = NP + P
    EDGE = 2

    with ExitStack() as ctx:
        def sb(name, shape, dt=F32):
            return ctx.enter_context(nc.sbuf_tensor(name, shape, dt))

        def sem(name):
            return ctx.enter_context(nc.semaphore(name))

        def dram(name, shape, dt=F32):
            return nc.dram_tensor(name, shape, dt).ap()

        rec_d = dram("rec_d", (STEPS, 4, P), I32)
        attr_d = dram("attr_d", (STEPS, P * EA))
        start_d = dram("start_d", (STEPS,))
        q_d = dram("q_d", (STEPS, 1))
        blk_d = dram("blk_d", (STEPS,), I32)
        rel_d = dram("rel_d", (STEPS, P))
        attr_s = dram("attr_s", (NG, P, G * EA))
        tab0 = dram("tab0", (NP, D))
        tab1 = dram("tab1", (NP, NREL * D))
        acc_d = [[dram(f"acc_d{m}_{t}", (ACC_ROWS, D)) for t in range(NT)] for m in range(NH)]
        src_d = dram("src_d", (STEPS, P))
        tab3 = dram("tab3", (NP, 2 * D))

        X = sb("X", [P, NB * D])
        H = sb("H", [P, NB * DA])
        TMP = sb("TMP", [P, NB * D])
        AG = sb("AG", [P, NB * D])
        Xv = X[:].rearrange("p (b f) -> p b f", f=D)
        Hv = H[:].rearrange("p (b f) -> p b f", f=DA)[:, :, 0:D]
        Hone = H[:].rearrange("p (b f) -> p b f", f=DA)[:, :, D:DA]
        TMPv = TMP[:].rearrange("p (b f) -> p b f", f=D)
        AGv = AG[:].rearrange("p (b f) -> p b f", f=D)
        s1 = sb("s1", [P, NB])
        s2 = sb("s2", [P, NB])
        s3 = sb("s3", [P, NB])
        srcT = sb("srcT", [P, STEPS], I32)
        rowT = sb("rowT", [P, STEPS], I32)
        relT = sb("relT", [P, STEPS])
        wT = sb("wT", [P, STEPS])
        blkR = sb("blkR", [1, STEPS], I32)
        idx = sb("idx", [P, R, G], I32)
        gat = sb("gat", [P, R, G * 2 * D])
        S = sb("S", [P, 2, G, P])
        ST = sb("ST", [P, 2, G, P])
        attrG = sb("attrG", [P, 2, G * EA])
        attrT = sb("attrT", [G * EA, P])
        pre = sb("pre", [P, G * D])
        h1 = sb("h1", [P, G * D])
        h1r = sb("h1r", [P, G * D])
        h2 = sb("h2", [2 * H2, G * D])
        h2r = sb("h2r", [2 * H2, G * D])
        esc = sb("esc", [P, G])
        dups = sb("dups", [P, G])
        away = sb("away", [P, G])
        junkP = sb("junkP", [P, 1])
        TO = sb("TO", [P, BG * NREL * D])
        HS = sb("HS", [P, BG * DA])
        HT = sb("HT", [DA, BG * P])
        iotaN = sb("iotaN", [P, P])
        iotaI = sb("iotaI", [P, P], I32)
        iotaP = sb("iotaP", [P, 1])
        iotaPi = sb("iotaPi", [P, 1], I32)
        ident = sb("ident", [P, P])
        stepN = sb("stepN", [P, NC])
        lower = sb("lower", [P, P])
        linB = sb("linB", [DA, NBASE])
        W0 = sb("W0", [DA, 2 * D])
        WR = sb("WR", [D, NREL * D])
        As = sb("As", [D, DA])
        At = sb("At", [D, DA])
        Ae = sb("Ae", [D, EA])
        be = sb("be", [D, 1])
        W1n = sb("W1n", [D, 3 * D])
        W1t = sb("W1t", [D, 4 * D])
        W2n = sb("W2n", [2 * H2, P])
        W3n = sb("W3n", [2, 2 * H2])
        W2t = sb("W2t", [P, 2 * H2])
        W3t = sb("W3t", [2 * H2, 2])
        W4 = sb("W4", [DA, 4 * D])
        We = sb("We", [EA, D])
        Web = sb("Web", [G * EA, G, D])
        b1c = sb("b1c", [P, 1])
        b1s = sb("b1s", [P, 1])
        b2c = sb("b2c", [2 * H2, 1])
        b3c = sb("b3c", [P, 1])
        dstI = TO[:, 0:STEPS].bitcast(I32)
        srcI = TO[:, STEPS:2 * STEPS].bitcast(I32)
        wI = AG[:, 0:STEPS].bitcast(I32)
        tyI = AG[:, STEPS:2 * STEPS].bitcast(I32)
        startB = H[:, 0:STEPS]
        leq = TMP[:, 0:STEPS]
        blo = sb("blo", [P, NC])
        cnt = sb("cnt", [P, NC])
        edgeB = sb("edgeB", [P, 2, NC], I32)
        start = sb("start", [P, NC])
        q = sb("q", [P, NC])
        tot = sb("tot", [P, 1])
        tile_i = sb("tile_i", [P, NC], I32)
        tcol = sb("tcol", [P, 1], I32)
        rg = gat[:, 0, 0:4 * P].bitcast(I32)
        eg = gat[:, 1, :]
        qg = sb("qg", [P, 1])
        nblk = sb("nblk", [P, 1])
        blkf = sb("blkf", [P, 1])
        blki = sb("blki", [P, 1], I32)
        stepc = sb("stepc", [P, 1])
        fld = gat[:, 2, 0:4 * P]
        eo = gat[:, 3, :]

        ps = [ctx.enter_context(nc.psum_tensor(f"ps{i}", [P, 512], F32)) for i in range(8)]

        SEMS = """gathers_begun turns_begun zero_ok pool_const const_ok edges_in lin_in w_in w0_ok rel_in mlp_in mlp_const mlp_T mlp_Tc
            mlp_mm mlp_c web_in rec_out attr_out attr_tail q_out start_in base_mm tcol_ok stair_g stair_f
            stair_T stair_e stair_out tiles_ok blk_in stair_done dve stair_d x_in ln_var ln_std ln_ok hs_ok
            hT_ps ht_ok proj_ps proj_mv proj_sb tab_out nrm_in nrm_out tabs_zero hop_go dst_ok msg_ps msg_ok sum_ps rows_ok dup_ok sum_mv idx_ok mm_ok S_ok acc_ok
            esc_ok ST_ok aT_ps aT_ok pre_ps pre_ok h1_ps h1_sb h1_ok h2_ps h2_sb h2_ok e_ps ge_ok out_ok pass_ok out_in
            """.split()
        sems = {n: sem(n) for n in SEMS}
        stp_in = [sem(f"stp_in{h}") for h in range(2)]
        gather_ok = [sem(f"gather_ok{r}") for r in range(R)]

        scat_ok = [sem(f"scat_ok{h}") for h in range(2)]
        rows_in = [sem(f"rows_in{h}") for h in range(2)]
        sum_in = [sem(f"sum_in{h}") for h in range(2)]

        block = ctx.enter_context(nc.Block())
        s_ = sems
        FULL = E // STEPS
        REST = E - FULL * STEPS
        NFULL = N // P
        PZ = next(u for u in range(1, 64) if ACC_ROWS % (P * u) == 0 and ACC_ROWS // (P * u) <= G)
        NREST = N - NFULL * P
        tail = STEPS * P * EA - E * EA
        assert tail % 16 == 0 and NB * D * 16 < tail <= 2 * NB * D * 16 and (E * EA) % 880 == 0

        def wait(eng, semaphore, value):
            if not isinstance(value, int) or value > 0:
                eng.wait_ge(semaphore, value)

        def turns(eng, n, body):
            body(0)
            with eng.Fori(1, n - 1) as i:
                body(i)
            body(n - 1)

        @block.sync
        def _(sp):
            sp.wait_ge(s_["zero_ok"], 1)
            for dstb, a in ((dstI, dst), (srcI, src), (wI, eweight.bitcast(I32)), (tyI, etype)):
                sp.dma_start(dstb[0:FULL, :], a[0:FULL * STEPS].rearrange("(p j) -> p j", j=STEPS)).then_inc(s_["edges_in"], 16)
                sp.dma_start(dstb[FULL:FULL + 1, 0:REST], a[FULL * STEPS:E].rearrange("(p j) -> p j", p=1)).then_inc(s_["edges_in"], 16)
            flat = attr_d.rearrange("t j -> (t j)")
            sp.dma_start(flat[0:E * EA].rearrange("(a b) -> a b", a=880),
                         edge_attr.rearrange("e a -> (e a)").rearrange("(a b) -> a b", a=880)).then_inc(s_["attr_out"], 16)
            for a0, a1 in ((0, NB * D * 16), (NB * D * 16, tail)):
                sp.dma_start(flat[E * EA + a0:E * EA + a1].rearrange("(a b) -> a b", a=16),
                             X[0:16, 0:(a1 - a0) // 16]).then_inc(s_["attr_tail"], 16)
            for half, (wt, bias) in enumerate(((msg_wt, msg_b), (self_wt, self_b))):
                wv = srcT if half == 0 else rowT
                sp.dma_start(wv[0:D, 0:D * NBASE].bitcast(F32), wt.rearrange("i o b -> i (o b)")).then_inc(s_["w_in"], 16)
                sp.dma_start(wv[D:DA, 0:D * NBASE].bitcast(F32), bias.rearrange("(u o) b -> u (o b)", u=1)).then_inc(s_["w_in"], 16)
            sp.dma_start(linB[:], lin.to_broadcast([DA, NBASE])).then_inc(s_["w_in"], 16)
            sp.dma_start(WR[:].rearrange("i (r o) -> i r o", r=NREL), rel_w.rearrange("r i o -> i r o")).then_inc(s_["rel_in"], 16)
            col = lambda a: a.rearrange("(p u) -> p u", u=1)
            sp.wait_ge(s_["zero_ok"], 2)
            for o, i in ((As[:, 0:D], W_src), (As[:, D:DA], col(b_src)), (At[:, 0:D], W_tgt), (At[:, D:DA], col(b_tgt)),
                         (Ae[:], W_edge), (be[:], col(b_edge)), (W1n[:], W1),
                         (W2n[0:H2, 0:D], W2), (W2n[H2:2 * H2, D:P], W2),
                         (W3n[0:1, 0:H2], W3), (W3n[1:2, H2:2 * H2], W3),
                         (b1s[0:D, :], col(b1)), (b1s[D:P, :], col(b1)), (b2c[0:H2, :], col(b2)), (b2c[H2:2 * H2, :], col(b2)),
                         (b3c[:], b3.rearrange("(u v) -> u v", u=1).to_broadcast([P, 1]))):
                sp.dma_start(o, i).then_inc(s_["mlp_in"], 16)
            sp.wait_ge(s_["edges_in"], 16 * 8)
            for f, b in enumerate((srcI, dstI, wI, tyI)):
                sp.dma_start(rec_d.rearrange("(p c) f j -> p c f j", c=NC)[:, :, f, :],
                             b.rearrange("p (c j) -> p c j", j=P)).then_inc(s_["rec_out"], 16)
            sp.wait_ge(s_["tiles_ok"], 1)
            sp.dma_start(start_d.rearrange("(p c) -> p c", c=NC), start[:]).then_inc(s_["q_out"], 16)
            sp.dma_start(q_d.rearrange("(p c) u -> p (c u)", c=NC), q[:]).then_inc(s_["q_out"], 16)
            sp.wait_ge(s_["q_out"], 32)
            sp.dma_start(startB, start_d.rearrange("(u s) -> u s", u=1).to_broadcast([P, STEPS])).then_inc(s_["start_in"], 16)
            with sp.Fori(0, NC) as c:
                sp.wait_ge(s_["stair_f"], c + 1)
                sp.dma_start(rel_d[bass.ds(c * P, P), :], fld[:, P:2 * P]).then_inc(s_["stair_out"], 16)
                sp.dma_start(src_d[bass.ds(c * P, P), :], fld[:, 0:P]).then_inc(s_["stair_out"], 16)
                sp.dma_start(blk_d[bass.ds(c * P, P)].rearrange("(p u) -> p u", u=1), blki[:]).then_inc(s_["stair_out"], 16)
                sp.wait_ge(s_["stair_e"], c + 1)
                sp.dma_start(attr_s[bass.ds(c * (P // G), P // G), :, :].rearrange("g p m -> p g m"),
                             eo.rearrange("p (g m) -> p g m", m=G * EA)).then_inc(s_["stair_out"], 16)
            sp.wait_ge(s_["stair_out"], 64 * NC)
            sp.dma_start(blkR[:], blk_d.rearrange("(u s) -> u s", u=1)).then_inc(s_["blk_in"], 16)
            sp.wait_ge(s_["attr_tail"], 32)
            sp.dma_start(Xv[:, 0:NFULL, :], x[0:NFULL * P, :].rearrange("(b p) f -> p b f", p=P)).then_inc(s_["x_in"], 16)
            sp.dma_start(Xv[0:NREST, NFULL, :], x[NFULL * P:N, :]).then_inc(s_["x_in"], 16)
            for k in range(G):
                if k == 0:
                    sp.wait_ge(s_["mlp_c"], 3)
                sp.dma_start(Web[k * EA:(k + 1) * EA, k, :], We[:]).then_inc(s_["web_in"], 16)

            def tables(n, tab, width):
                with sp.Fori(0, NJ) as j:
                    sp.wait_ge(s_["proj_sb"], j + n * NJ + 1)
                    sp.dma_start(tab.rearrange("(b p) f -> p b f", p=P)[:, bass.ds(j * BG, BG), :],
                                 TO[:, 0:BG * width].rearrange("p (b f) -> p b f", f=width)).then_inc(s_["tab_out"], 16)

            tables(0, tab0, D)
            sp.wait_ge(s_["zero_ok"], 2)
            for m in range(NH):
                for t in range(NT):
                    sp.dma_start(acc_d[m][t].rearrange("(p u b) f -> p u (b f)", p=P, u=PZ),
                                 pre[:, 0:ACC_ROWS * D // (P * PZ)].rearrange("p (v w) -> p v w", v=1).to_broadcast([P, PZ, ACC_ROWS * D // (P * PZ)])).then_inc(s_["tabs_zero"], 16)
            tables(1, tab1, NREL * D)
            for m in range(NH):
                sp.wait_ge(s_["hop_go"], 2 * m + 1)

                def rows(i):
                    for h in range(2):
                        g = i * 2 + h
                        wait(sp, s_["sum_ps"], m * NG + g - 1)
                        sp.dma_start(ST[:, h, :, :].rearrange("p k e -> p (k e)"),
                                     rel_d[bass.ds(g * G, G), :].rearrange("(u k) e -> u (k e)", u=1).to_broadcast([P, G * P])).then_inc(rows_in[h], 16)
                        sp.dma_start(S[:, h, :, :].rearrange("p k e -> p (k e)"),
                                     src_d[bass.ds(g * G, G), :].rearrange("(u k) e -> u (k e)", u=1).to_broadcast([P, G * P])).then_inc(rows_in[h], 16)

                turns(sp, NG // 2, rows)
                for h in range(2):
                    sp.wait_ge(scat_ok[h], (m + 1) * NG * 16 * (G // 2))
                sp.wait_ge(s_["hop_go"], 2 * m + 2)
                for t in range(NT):
                    if t >= 2:
                        sp.wait_ge(s_["sum_mv"], m * NT + t - 1)
                    sp.dma_start((TMPv, TO[:, 0:NB * D].rearrange("p (b f) -> p b f", f=D))[t % 2],
                                 acc_d[m][t][0:NP, :].rearrange("(b p) f -> p b f", p=P)).then_inc(sum_in[t % 2], 16)
            tables(2, tab3, 2 * D)
            with sp.Fori(0, NG // 2) as i:
                for h in range(2):
                    sp.wait_ge(s_["out_ok"], i * 2 + h + 1)
                    sp.dma_start(ST[:, h, :, :].rearrange("p k e -> p (k e)"),
                                 rel_d[bass.ds(i * (2 * G) + h * G, G), :].rearrange("(u k) e -> u (k e)", u=1).to_broadcast([P, G * P])).then_inc(stp_in[h], 16)
                    sp.dma_start(attrG[:, h, :], attr_s[bass.ds(i * 2 + h, 1), :, :].rearrange("g p m -> (g p) m")).then_inc(stp_in[h], 16)
            sp.wait_ge(s_["pass_ok"], 1)
            sp.dma_start(out[0:NFULL * P, :].rearrange("(b p) f -> p b f", p=P), Xv[:, 0:NFULL, :]).then_inc(s_["out_in"], 16)
            sp.dma_start(out[NFULL * P:N, :], Xv[0:NREST, NFULL, :]).then_inc(s_["out_in"], 16)
            sp.wait_ge(s_["out_in"], 32)

        @block.gpsimd
        def _(pool):
            pool.iota(iotaI[:], [[1, P]], base=0, channel_multiplier=0).then_inc(s_["pool_const"], 1)
            pool.iota(iotaPi[:], [[0, 1]], base=0, channel_multiplier=1).then_inc(s_["pool_const"], 1)
            pool.memset(ident[:], 0.0).then_inc(s_["pool_const"], 1)
            pool.memset(lower[:], 1.0).then_inc(s_["pool_const"], 1)
            pool.wait_ge(s_["pool_const"], 4)
            pool.affine_select(out=ident[:], in_=ident[:], compare_op=ALU.not_equal, fill=1.0, base=0,
                               pattern=[[-1, P]], channel_multiplier=1).then_inc(s_["pool_const"], 1)
            pool.affine_select(out=lower[:], in_=lower[:], compare_op=ALU.is_gt, fill=0.0, base=0,
                               pattern=[[1, P]], channel_multiplier=-1).then_inc(s_["pool_const"], 1)
            pool.iota(tile_i[:], [[P, NC]], base=0, channel_multiplier=1).then_inc(s_["pool_const"], 1)
            pool.wait_ge(s_["rec_out"], 64)
            pool.wait_ge(s_["attr_out"], 16)
            pool.wait_ge(s_["attr_tail"], 32)
            with pool.Fori(0, NC) as c:
                pool.wait_ge(s_["tcol_ok"], c + 1)
                pool.sem_inc(s_["gathers_begun"], 1)
                off = bass.IndirectOffsetOnAxis(ap=tcol[:], axis=0)
                pool.indirect_dma_start(rg, None, rec_d.rearrange("t f j -> t (f j)"), off).then_inc(s_["stair_g"], 16)
                pool.indirect_dma_start(eg, None, attr_d, off).then_inc(s_["stair_g"], 16)
                pool.indirect_dma_start(qg[:], None, q_d, off).then_inc(s_["stair_g"], 16)

            def gathers(n, table, width):
                with pool.Fori(0, NG // R) as i:
                    for r in range(R):
                        pool.wait_ge(s_["idx_ok"], i * R + n * NG + r + 1)
                        pool.sem_inc(s_["gathers_begun"], 1)
                        for k in range(G):
                            pool.indirect_dma_start(gat[:, r, k * width:(k + 1) * width], None, table,
                                                    bass.IndirectOffsetOnAxis(ap=idx[:, r, k:k + 1], axis=0)).then_inc(gather_ok[r], 16)

            pool.wait_ge(s_["tab_out"], 16 * NJ)
            gathers(0, tab0, D)
            pool.wait_ge(s_["tab_out"], 32 * NJ)
            gathers(1, tab1.rearrange("n (r f) -> (n r) f", f=D), D)
            pool.wait_ge(s_["tabs_zero"], 16 * NH * NT)
            for m in range(NH):
                def scatters(i):
                    for r in range(R):
                        g = i * R + r
                        pool.wait_ge(s_["rows_ok"], m * NG + g + 1)
                        if not isinstance(g, int):
                            pool.sem_inc(s_["gathers_begun"], 1)
                        for k in range(G):
                            if k % (G // 2) == 0:
                                h = k // (G // 2)
                                wait(pool, scat_ok[h], (m * NG + g) * 16 * (G // 2))
                                if not isinstance(g, int):
                                    pool.sem_inc(s_["gathers_begun"], 1)
                            pool.indirect_dma_start(acc_d[m][k], bass.IndirectOffsetOnAxis(ap=idx[:, r, k:k + 1], axis=0),
                                                    gat[:, r, k * D:(k + 1) * D], None, compute_op=ALU.add).then_inc(scat_ok[k // (G // 2)], 16)

                turns(pool, NG // R, scatters)
            pool.wait_ge(s_["tab_out"], 48 * NJ)
            gathers(EDGE, tab3, 2 * D)

        @block.scalar
        def _(act):
            act.wait_ge(s_["mlp_T"], 1)
            act.copy(W1t[:], ps[0][0:D, 0:4 * D]).then_inc(s_["mlp_Tc"], 1)
            act.copy(W2t[:], ps[1][:, 0:2 * H2]).then_inc(s_["mlp_Tc"], 1)
            act.copy(W3t[:], ps[1][0:2 * H2, P:P + 2]).then_inc(s_["mlp_Tc"], 1)
            act.wait_ge(s_["mlp_mm"], 1)
            act.wait_ge(s_["zero_ok"], 2)
            act.copy(W4[:], ps[2][0:DA, 0:4 * D]).then_inc(s_["mlp_c"], 1)
            act.activation(b1c[:], ps[3][:, 0:1], ACT.Identity, bias=b1s[:, 0:1]).then_inc(s_["mlp_c"], 1)
            act.copy(We[:], ps[3][0:EA, D:2 * D]).then_inc(s_["mlp_c"], 1)
            def attributes(c):
                act.wait_ge(s_["stair_T"], c + 1)
                wait(act, s_["stair_out"], c * 64)
                for hb in range(2):
                    o = eo.rearrange("p (s a) -> p a s", a=EA)[:, 4 * hb:4 * hb + 4, :]
                    ins = act.copy(o, ps[5 + hb][:].rearrange("p (a s) -> p a s", a=4))
                ins.then_inc(s_["stair_e"], 1)

            turns(act, NC, attributes)

            def std(n):
                act.wait_ge(s_["ln_var"], n)
                act.activation(s3[:], s2[:], ACT.Sqrt).then_inc(s_["ln_std"], 1)

            def turn(n):
                def group(j):
                    wait(act, s_["hT_ps"], j + n * NJ)
                    act.copy(HS[:], H[:, bass.ds(j * (BG * DA), BG * DA)]).then_inc(s_["hs_ok"], 1)
                    act.wait_ge(s_["hT_ps"], j + n * NJ + 1)
                    act.copy(HT[:], ps[0][0:DA, :]).then_inc(s_["ht_ok"], 1)

                turns(act, NJ, group)

            def indices(n, table):
                with act.Fori(0, NG // R) as i:
                    for r in range(R):
                        act.wait_ge(s_["mm_ok"], i * R + n * NG + r + 1)
                        act.copy(idx[:, r, :], table[:, bass.ds(i * (R * G) + r * G, G)]).then_inc(s_["idx_ok"], 1)

            std(1)
            act.wait_ge(s_["ln_ok"], 1)
            turn(0)
            act.wait_ge(s_["stair_done"], 1)
            indices(0, srcT)
            act.wait_ge(s_["nrm_in"], 1)
            act.activation(s3[:], s2[:], ACT.Sqrt).then_inc(s_["nrm_out"], 1)
            std(2)
            act.wait_ge(s_["ln_ok"], 2)
            turn(1)
            indices(1, rowT)
            std(3)
            for m in range(NH):
                def out_rows(i):
                    for r in range(R):
                        g = i * R + r
                        act.wait_ge(s_["sum_ps"], m * NG + g + 1)
                        for h in range(2):
                            wait(act, scat_ok[h], (m * NG + g - R + 1) * 16 * (G // 2))
                        act.copy(idx[:, r, :], rowT[:, bass.ds(g * G, G)])
                        act.copy(gat[:, r, 0:G * D], ps[2 + r % 2][:]).then_inc(s_["rows_ok"], 1)

                turns(act, NG // R, out_rows)
            std(4)
            act.wait_ge(s_["ln_ok"], 4)
            turn(2)
            for r in range(R):
                act.wait_ge(s_["mm_ok"], EDGE * NG + r + 1)
                act.copy(idx[:, r, :], srcT[:, r * G:(r + 1) * G]).then_inc(s_["idx_ok"], 1)

            def mlp_group(g, r, last):
                act.wait_ge(s_["aT_ps"], g + 1)
                act.copy(attrT[:], ps[0][0:G * EA, 0:P]).then_inc(s_["aT_ok"], 1)
                act.wait_ge(s_["h1_ps"], g + 1)
                act.activation(h1[:], ps[2][:], ACT.Identity, bias=b1c[:, 0:1]).then_inc(s_["h1_sb"], 1)
                act.wait_ge(s_["h2_ps"], g + 1)
                act.activation(h2[:], ps[3][0:2 * H2, :], ACT.Identity, bias=b2c[:, 0:1]).then_inc(s_["h2_sb"], 1)
                if not last:
                    act.wait_ge(s_["mm_ok"], g + (EDGE * NG + R + 1))
                    act.copy(idx[:, r, :], srcT[:, bass.ds(g * G + R * G, G)]).then_inc(s_["idx_ok"], 1)

            with act.Fori(0, NG // R - 1) as i:
                for r in range(R):
                    mlp_group(i * R + r, r, False)
            for r in range(R):
                mlp_group(NG - R + r, r, True)

        @block.tensor
        def _(pe):
            pe.wait_ge(s_["const_ok"], 1)
            pe.sem_inc(s_["mm_ok"], R)
            pe.wait_ge(s_["mlp_in"], 16 * 16)
            for k in range(4):
                pe.transpose(ps[0][0:D, k * D:(k + 1) * D], W1n[:, min(k, 2) * D:min(k, 2) * D + D], ident[0:D, 0:D])
            pe.transpose(ps[1][:, 0:2 * H2], W2n[:], ident[0:2 * H2, 0:2 * H2])
            pe.transpose(ps[1][0:2 * H2, P:P + 2], W3n[:], ident[0:2, 0:2])
            pe.transpose(ps[2][0:DA, 0:D], As[:], ident[0:D, 0:D])
            pe.transpose(ps[2][0:DA, 2 * D:3 * D], At[:], ident[0:D, 0:D]).then_inc(s_["mlp_T"], 1)
            pe.wait_ge(s_["mlp_Tc"], 3)
            pe.matmul(ps[2][0:DA, D:2 * D], As[:], W1t[:, 0:D], start=True, stop=True)
            pe.matmul(ps[2][0:DA, 3 * D:4 * D], At[:], W1t[:, D:2 * D], start=True, stop=True)
            pe.matmul(ps[3][:, 0:1], W1t[:, 2 * D:4 * D], be[:], start=True, stop=True)
            pe.matmul(ps[3][0:EA, D:2 * D], Ae[:], W1t[:, 2 * D:3 * D], start=True, stop=True).then_inc(s_["mlp_mm"], 1)
            pe.wait_ge(s_["base_mm"], 1)
            pe.matmul(ps[4][:, 0:1], lower[:], tot[:], start=True, stop=True).then_inc(s_["base_mm"], 1)
            def columns(c):
                pe.wait_ge(s_["stair_f"], c + 1)
                for f in range(4):
                    src_ap = fld[:, f * P:(f + 1) * P] if f != 2 else rg[:, 2 * P:3 * P].bitcast(F32)
                    pe.transpose(ps[4][:, f * P:(f + 1) * P], src_ap, ident[:])
                wait(pe, s_["stair_e"], c)
                for a in range(EA):
                    ins = pe.transpose(ps[5 + a // 4][:, (a % 4) * P:(a % 4 + 1) * P],
                                       eg.rearrange("p (e a) -> p a e", a=EA)[:, a, :], ident[:])
                ins.then_inc(s_["stair_T"], 1)

            turns(pe, NC, columns)

            def project(n, w, width, k):
                def group(j):
                    pe.wait_ge(s_["hs_ok"], j + n * NJ + 1)
                    for b in range(BG):
                        ins = pe.transpose(ps[0][0:DA, b * P:(b + 1) * P], HS[:, b * DA:(b + 1) * DA], ident[:])
                    ins.then_inc(s_["hT_ps"], 1)
                    pe.wait_ge(s_["ht_ok"], j + n * NJ + 1)
                    for b in range(BG):
                        bank = 2 + 2 * (b % 2)
                        wait(pe, s_["proj_mv"], (j + n * NJ) * BG + max(b - 1, 0))
                        for w0 in range(0, width, 512):
                            m = min(512, width - w0)
                            ins = pe.matmul(ps[bank + w0 // 512][:, 0:m], HT[0:k, b * P:(b + 1) * P], w[0:k, w0:w0 + m],
                                            start=True, stop=True)
                        ins.then_inc(s_["proj_ps"], 1)

                turns(pe, NJ, group)

            def segment(n):
                def groups(i):
                    for r in range(R):
                        pe.wait_ge(gather_ok[r], i * (16 * G) + (n * (NG // R) + 1) * 16 * G)
                        pe.wait_ge(s_["S_ok"], i * R + n * NG + r + 1)
                        wait(pe, s_["acc_ok"], (i * R + n * NG + r - 1) * G)
                        for k in range(G):
                            ins = pe.matmul(ps[6 + r % 2][:, k * D:(k + 1) * D], S[:, r % 2, k, :], gat[:, r, k * D:(k + 1) * D],
                                            start=True, stop=True)
                        ins.then_inc(s_["mm_ok"], 1)

                turns(pe, NG // R, groups)

            pe.wait_ge(s_["mlp_c"], 3)
            pe.wait_ge(s_["stair_e"], NC)
            pe.wait_ge(s_["stair_done"], 1)
            pe.wait_ge(s_["w0_ok"], 1)
            project(0, W0, 2 * D, DA)
            segment(0)
            pe.wait_ge(s_["rel_in"], 16)
            project(1, WR, NREL * D, D)
            segment(1)
            regs = [pe.alloc_register(f"pe_blk{k}") for k in range(G)]

            def spread(bank, g, h, stop):
                pe.reg_load(regs, blkR[0:1, bass.ds(g * G, G)])
                cols = [pe.snap(x_, min_val=0, max_val=(NODE_BLOCKS - 1) * D) for x_ in regs]
                for k in range(G):
                    ins = pe.matmul(ps[bank][:, k * D:(k + 1) * D], ST[:, h, k, :], AG[:, bass.ds(cols[k], D)],
                                    start=True, stop=stop)
                    if not stop:
                        ins = pe.matmul(ps[bank][:, k * D:(k + 1) * D], attrT[:], Web[:, k, :], start=False, stop=True)
                return ins

            for m in range(NH):
                def hops(i):
                    for r in range(R):
                        g, h = i * R + r, r % 2
                        pe.wait_ge(s_["dst_ok"], m * NG + g + 1)
                        spread(h, g, h, True).then_inc(s_["msg_ps"], 1)
                        pe.wait_ge(s_["msg_ok"], m * NG + g + 1)
                        wait(pe, s_["rows_ok"], m * NG + g - 1)
                        for k in range(G):
                            ins = pe.matmul(ps[2 + h][:, k * D:(k + 1) * D], S[:, h, k, :], pre[:, k * D:(k + 1) * D],
                                            start=True, stop=True)
                        ins.then_inc(s_["sum_ps"], 1)

                turns(pe, NG // R, hops)
            project(2, W4, 4 * D, DA)
            pe.wait_ge(s_["web_in"], 16 * G)

            def edges(i):
                for r in range(R):
                    h = r % 2
                    g = i * R + r
                    pe.wait_ge(s_["ST_ok"], g + 1)
                    if not isinstance(g, int):
                        pe.sem_inc(s_["turns_begun"], 1)
                    pe.transpose(ps[0][0:G * EA, 0:P], attrG[:, h, :], ident[:]).then_inc(s_["aT_ps"], 1)
                    pe.wait_ge(s_["aT_ok"], g + 1)
                    spread(1, g, h, False).then_inc(s_["pre_ps"], 1)
                    pe.wait_ge(s_["pre_ok"], g + 1)
                    for k in range(G // 2):
                        ins = pe.transpose(ps[2][:, k * P:(k + 1) * P], pre[:, k * P:(k + 1) * P], ident[:])
                    ins.then_inc(s_["h1_ps"], 1)
                    pe.wait_ge(s_["h1_ok"], g + 1)
                    pe.matmul(ps[3][0:2 * H2, :], W2t[:], h1r[:], start=True, stop=True).then_inc(s_["h2_ps"], 1)
                    pe.wait_ge(s_["h2_ok"], g + 1)
                    for k in range(G // 2):
                        ins = pe.matmul(ps[4][:, 2 * k:2 * k + 2], h2r[:, k * P:(k + 1) * P], W3t[:], start=True, stop=True)
                    ins.then_inc(s_["e_ps"], 1)
                    pe.wait_ge(s_["ge_ok"], g + 1)
                    pe.wait_ge(s_["S_ok"], g + EDGE * NG + 1)
                    pe.wait_ge(s_["acc_ok"], (g + EDGE * NG - 1) * G)
                    for k in range(G):
                        ins = pe.matmul(ps[6 + h][:, k * D:(k + 1) * D], S[:, h, k, :], gat[:, r, k * 2 * D:k * 2 * D + D],
                                        start=True, stop=True)
                    ins.then_inc(s_["mm_ok"], 1)

            turns(pe, NG // R, edges)

        @block.vector
        def _(dve):
            steps = [0]

            def chain(ins):
                steps[0] += 1
                ins.then_inc(s_["dve"], 1)
                dve.wait_ge(s_["dve"], steps[0])

            def wide(a):
                return a[:].rearrange("p (b u) -> p b u", u=1).to_broadcast([P, NB, D])

            dve.memset(X[:], 0.0)
            dve.memset(dstI, PAD_DST)
            dve.memset(srcI, 0)
            dve.memset(wI, 0)
            chain(dve.memset(tyI, 0))
            dve.sem_inc(s_["zero_ok"], 1)
            dve.memset(pre[:], 0.0)
            dve.memset(W2n[:], 0.0)
            dve.memset(W3n[:], 0.0)
            chain(dve.memset(Web[:], 0.0))
            dve.sem_inc(s_["zero_ok"], 1)
            dve.wait_ge(s_["pool_const"], 7)
            dve.tensor_copy(iotaN[:], iotaI[:])
            chain(dve.tensor_copy(iotaP[:], iotaPi[:]))
            dve.tensor_scalar(junkP[:], iotaP[:], float(NP), None, ALU.add)
            chain(dve.tensor_copy(stepN[:], tile_i[:]))
            dve.sem_inc(s_["const_ok"], 1)
            dve.wait_ge(s_["w_in"], 16 * 5)
            for half, wv in enumerate((srcT, rowT)):
                v = wv[0:DA, 0:D * NBASE].bitcast(F32).rearrange("i (o b) -> i o b", b=NBASE)
                c3 = linB[:].rearrange("i (u b) -> i u b", u=1).to_broadcast([DA, D, NBASE])
                chain(dve.tensor_tensor(v, v, c3, ALU.mult))
                chain(dve.tensor_reduce(W0[:, half * D:(half + 1) * D], v, AX.X, ALU.add))
            dve.sem_inc(s_["w0_ok"], 1)
            dve.wait_ge(s_["edges_in"], 16 * 8)
            dv = dstI.rearrange("p (c j) -> p c j", j=P)
            dve.tensor_scalar(edgeB[:, 0, :], dv[:, :, 0], 7, None, ALU.logical_shift_right)
            chain(dve.tensor_scalar(edgeB[:, 1, :], dv[:, :, P - 1], 7, None, ALU.logical_shift_right))
            chain(dve.tensor_copy(blo[:], edgeB[:, 0, :]))
            chain(dve.tensor_copy(cnt[:], edgeB[:, 1, :]))
            chain(dve.scalar_tensor_tensor(cnt[:], cnt[:], 1.0, blo[:], ALU.add, ALU.subtract))
            chain(dve.tensor_reduce(tot[:], cnt[:], AX.X, ALU.add))
            dve.sem_inc(s_["base_mm"], 1)
            dve.wait_ge(s_["base_mm"], 2)
            chain(dve.tensor_copy(start[:, 0:1], ps[4][:, 0:1]))
            for c in range(1, NC):
                chain(dve.tensor_tensor(start[:, c:c + 1], start[:, c - 1:c], cnt[:, c - 1:c], ALU.add))
            chain(dve.tensor_tensor(q[:], blo[:], start[:], ALU.subtract))
            dve.sem_inc(s_["tiles_ok"], 1)
            dve.wait_ge(s_["start_in"], 16)
            for c in range(NC):
                chain(dve.tensor_scalar(leq, startB, stepN[:, c:c + 1], None, ALU.is_le))
                chain(dve.tensor_reduce(cnt[:, c:c + 1], leq, AX.X, ALU.add))
            chain(dve.tensor_scalar(tile_i[:], cnt[:], -1.0, None, ALU.add))

            def columns(c):
                dve.tensor_copy(stepc[:], stepN[:, bass.ds(c, 1)])
                dve.tensor_copy(tcol[:], tile_i[:, bass.ds(c, 1)]).then_inc(s_["tcol_ok"], 1)
                dve.wait_ge(s_["tcol_ok"], c + 1)
                dve.wait_ge(s_["stair_g"], c * 48 + 48)
                wait(dve, s_["stair_out"], c * 64)
                dve.tensor_tensor(blkf[:], qg[:], stepc[:], ALU.add)
                dve.tensor_copy(fld[:, 0:P], rg[:, 0:P])
                dve.tensor_copy(fld[:, P:2 * P], rg[:, P:2 * P])
                dve.tensor_copy(fld[:, 3 * P:4 * P], rg[:, 3 * P:4 * P]).then_inc(s_["stair_d"], 1)
                dve.wait_ge(s_["stair_d"], c * 3 + 1)
                dve.tensor_scalar(blki[:], blkf[:], float(D), None, ALU.mult)
                dve.tensor_scalar(nblk[:], blkf[:], -float(P), None, ALU.mult)
                dve.scalar_tensor_tensor(fld[:, 3 * P:4 * P], fld[:, 0:P], float(NREL), fld[:, 3 * P:4 * P],
                                         ALU.mult, ALU.add).then_inc(s_["stair_d"], 1)
                dve.wait_ge(s_["stair_d"], c * 3 + 2)
                dve.tensor_scalar(fld[:, P:2 * P], fld[:, P:2 * P], nblk[:, 0:1], None, ALU.add).then_inc(s_["stair_f"], 1)
                dve.wait_ge(s_["stair_T"], c + 1)
                dve.tensor_copy(srcT[:, bass.ds(c * P, P)], ps[4][:, 0:P])
                dve.tensor_copy(relT[:, bass.ds(c * P, P)], ps[4][:, P:2 * P])
                dve.tensor_copy(wT[:, bass.ds(c * P, P)], ps[4][:, 2 * P:3 * P])
                dve.tensor_copy(rowT[:, bass.ds(c * P, P)], ps[4][:, 3 * P:4 * P]).then_inc(s_["stair_d"], 1)
                dve.wait_ge(s_["stair_d"], c * 3 + 3)

            turns(dve, NC, columns)
            dve.sem_inc(s_["stair_done"], 1)
            dve.wait_ge(s_["x_in"], 32)
            chain(dve.memset(H[:], 1.0))

            def layernorm(n):
                chain(dve.tensor_reduce(s1[:], Xv, AX.X, ALU.add))
                chain(dve.tensor_scalar(s1[:], s1[:], 1.0 / D, None, ALU.mult))
                chain(dve.tensor_tensor(Hv, Xv, wide(s1), ALU.subtract))
                chain(dve.tensor_tensor(TMPv, Hv, Hv, ALU.mult))
                chain(dve.tensor_reduce(s2[:], TMPv, AX.X, ALU.add))
                chain(dve.tensor_scalar(s2[:], s2[:], 1.0 / D, LN_EPS, ALU.mult, ALU.add))
                dve.sem_inc(s_["ln_var"], 1)
                dve.wait_ge(s_["ln_std"], n)
                chain(dve.reciprocal(s1[:], s3[:]))
                chain(dve.tensor_tensor(Hv, Hv, wide(s1), ALU.mult))
                chain(dve.tensor_scalar(Hv, Hv, 0.0, None, ALU.max))
                dve.sem_inc(s_["ln_ok"], 1)

            def projected(n, move):
                def group(j):
                    wait(dve, s_["tab_out"], (j + n * NJ) * 16)
                    for b in range(BG):
                        bank = 2 + 2 * (b % 2)
                        dve.wait_ge(s_["proj_ps"], (j + n * NJ) * BG + b + 1)
                        move(j, b, bank).then_inc(s_["proj_mv"], 1)
                    dve.wait_ge(s_["proj_mv"], (j + n * NJ) * BG + BG)
                    dve.sem_inc(s_["proj_sb"], 1)

                turns(dve, NJ, group)

            def move0(j, b, bank):
                dve.tensor_copy(TO[:, b * D:(b + 1) * D], ps[bank][:, 0:D])
                return dve.tensor_copy(AG[:, bass.ds(j * (BG * D) + b * D, D)], ps[bank][:, D:2 * D])

            def move1(j, b, bank):
                w = NREL * D
                dve.tensor_copy(TO[:, b * w:b * w + 512], ps[bank][:])
                return dve.tensor_copy(TO[:, b * w + 512:(b + 1) * w], ps[bank + 1][:])

            def move3(j, b, bank):
                dve.tensor_copy(TO[:, b * 2 * D:(b + 1) * 2 * D], ps[bank][:, 0:2 * D])
                xb = X[:, bass.ds(j * (BG * D) + b * D, D)]
                dve.tensor_tensor(xb, xb, ps[bank][:, 2 * D:3 * D], ALU.add)
                return dve.tensor_copy(AG[:, bass.ds(j * (BG * D) + b * D, D)], ps[bank][:, 3 * D:4 * D])

            def steps_of(t, g, width=P):
                return t[:, bass.ds(g * G, G)].rearrange("p (k u) -> p k u", u=1).to_broadcast([P, G, width])

            nview = iotaN[:].rearrange("p (u n) -> p u n", u=1).to_broadcast([P, G, P])

            def one_hot(n, g, h):
                wait(dve, s_["mm_ok"], n * NG + g + (R - 1))
                dve.tensor_tensor(S[:, h, :, :], steps_of(relT, g), nview, ALU.is_equal).then_inc(s_["S_ok"], 1)

            regs = [dve.alloc_register(f"dve_blk{k}") for k in range(G)]

            def accumulate(n, i, r, acc):
                dve.reg_load(regs, blkR[0:1, bass.ds(i * (R * G) + r * G, G)])
                cols = [dve.snap(x_, min_val=0, max_val=(NODE_BLOCKS - 1) * D) for x_ in regs]
                dve.wait_ge(s_["mm_ok"], i * R + (n * NG + r + R + 1))
                for k in range(G):
                    if k:
                        dve.wait_ge(s_["acc_ok"], i * (R * G) + (n * NG + r) * G + k)
                    a = acc[:, bass.ds(cols[k], D)]
                    dve.tensor_tensor(a, a, ps[6 + r % 2][:, k * D:(k + 1) * D], ALU.add).then_inc(s_["acc_ok"], 1)
                dve.wait_ge(s_["acc_ok"], i * (R * G) + (n * NG + r) * G + G)

            def message_pass(n, acc):
                one_hot(n, 0, 0)

                def groups(i):
                    for r in range(R):
                        g = i * R + r
                        if not (isinstance(g, int) and g == NG - 1):
                            one_hot(n, g + 1, (r + 1) % 2)
                        accumulate(n, i, r, acc)

                turns(dve, NG // R, groups)

            layernorm(1)
            projected(0, move0)
            dve.wait_ge(s_["blk_in"], 16)
            message_pass(0, AG)
            chain(dve.tensor_tensor(TMPv, AGv, AGv, ALU.mult))
            chain(dve.tensor_reduce(s2[:], TMPv, AX.X, ALU.add))
            dve.sem_inc(s_["nrm_in"], 1)
            dve.wait_ge(s_["nrm_out"], 1)
            chain(dve.tensor_scalar(s1[:], s3[:], L2_EPS, None, ALU.max))
            chain(dve.reciprocal(s1[:], s1[:]))
            chain(dve.tensor_tensor(AGv, AGv, wide(s1), ALU.mult))
            chain(dve.tensor_tensor(Xv, Xv, AGv, ALU.add))
            layernorm(2)
            projected(1, move1)
            message_pass(1, X)
            layernorm(3)
            dve.wait_ge(s_["tabs_zero"], 16 * NH * NT)
            chain(dve.tensor_copy(AGv, Hv))
            mask = lower[:].rearrange("p (u n) -> p u n", u=1).to_broadcast([P, G, P])
            for m in range(NH):
                dve.sem_inc(s_["hop_go"], 1)

                def matrices(g, i, r):
                    h = r % 2
                    dve.wait_ge(rows_in[h], (m * (NG // 2) + i * (R // 2) + r // 2 + 1) * 32)
                    dve.tensor_scalar(ST[:, h, :, :], ST[:, h, :, :], iotaP[:, 0:1], None, ALU.is_equal)
                    dve.tensor_tensor(S[:, h, :, :], S[:, h, :, :], steps_of(srcT, g), ALU.is_equal).then_inc(s_["dst_ok"], 1)

                def targets(g, h):
                    dve.wait_ge(s_["dst_ok"], g + 1)
                    wait(dve, s_["dup_ok"], g * 4)
                    later = TO[:, 0:G * P].rearrange("p (k e) -> p k e", k=G)
                    dve.tensor_tensor(later, S[:, h, :, :], mask, ALU.mult).then_inc(s_["dup_ok"], 1)
                    dve.tensor_scalar(away[:], srcT[:, bass.ds(g * G, G)], -1.0, junkP[:, 0:1], ALU.mult, ALU.add)
                    dve.wait_ge(s_["dup_ok"], g * 4 + 1)
                    dve.tensor_reduce(dups[:], later, AX.X, ALU.add).then_inc(s_["dup_ok"], 1)
                    dve.wait_ge(s_["dup_ok"], g * 4 + 2)
                    dve.scalar_tensor_tensor(away[:], dups[:], 0.5, away[:], ALU.is_gt, ALU.mult).then_inc(s_["dup_ok"], 1)
                    dve.wait_ge(s_["dup_ok"], g * 4 + 3)
                    dve.tensor_tensor(rowT[:, bass.ds(g * G, G)], away[:], srcT[:, bass.ds(g * G, G)], ALU.add).then_inc(s_["dup_ok"], 1)

                matrices(0, 0, 0)

                def groups(i):
                    for r in range(R):
                        g = i * R + r
                        if r < R - 1:
                            matrices(g + 1, i, r + 1)
                        elif not (isinstance(i, int) and i == NG // R - 1):
                            matrices(g + 1, i + 1, 0)
                        if m == 0:
                            targets(g, r % 2)
                        dve.wait_ge(s_["msg_ps"], m * NG + g + 1)
                        dve.tensor_tensor(pre[:].rearrange("p (k f) -> p k f", f=D), ps[r % 2][:].rearrange("p (k f) -> p k f", f=D),
                                          steps_of(wT, g, D), ALU.mult).then_inc(s_["msg_ok"], 1)

                turns(dve, NG // R, groups)
                dve.wait_ge(s_["sum_ps"], (m + 1) * NG)
                dve.sem_inc(s_["hop_go"], 1)
                for t in range(NT):
                    dve.wait_ge(sum_in[t % 2], (m * (NT // 2) + t // 2 + 1) * 16)
                    part = (TMP[:], TO[:, 0:NB * D])[t % 2]
                    if t == 0:
                        chain(dve.tensor_copy(AG[:], part))
                    else:
                        chain(dve.tensor_tensor(AG[:], AG[:], part, ALU.add))
                    dve.sem_inc(s_["sum_mv"], 1)
                chain(dve.tensor_tensor(Hv, Hv, AGv, ALU.add))
            chain(dve.scalar_tensor_tensor(Xv, Hv, 0.25, Xv, ALU.mult, ALU.add))
            layernorm(4)
            projected(2, move3)
            dve.sem_inc(s_["out_ok"], 2)
            one_hot(EDGE, 0, 0)

            def edges(i):
                for r in range(R):
                    g = i * R + r
                    h = r % 2
                    dve.wait_ge(stp_in[h], i * (16 * R) + (r // 2) * 32 + 32)
                    dve.tensor_scalar(ST[:, h, :, :], ST[:, h, :, :], iotaP[:, 0:1], None, ALU.is_equal).then_inc(s_["ST_ok"], 1)
                    if not (isinstance(g, int) and g == NG - 1):
                        one_hot(EDGE, g + 1, (r + 1) % 2)
                    dve.wait_ge(s_["pre_ps"], g + 1)
                    dve.wait_ge(gather_ok[r], i * (16 * G) + (EDGE * (NG // R) + 1) * 16 * G)
                    gv = gat[:, r, :].rearrange("p (k f) -> p k f", f=2 * D)
                    dve.tensor_tensor(pre[:].rearrange("p (k f) -> p k f", f=D), ps[1][:].rearrange("p (k f) -> p k f", f=D),
                                      gv[:, :, D:2 * D], ALU.add).then_inc(s_["pre_ok"], 1)
                    dve.wait_ge(s_["h1_sb"], g + 1)
                    dve.scalar_tensor_tensor(h1r[:], h1[:], NEG_SLOPE, h1[:], ALU.mult, ALU.max).then_inc(s_["h1_ok"], 1)
                    dve.wait_ge(s_["h2_sb"], g + 1)
                    dve.scalar_tensor_tensor(h2r[:], h2[:], NEG_SLOPE, h2[:], ALU.mult, ALU.max).then_inc(s_["h2_ok"], 1)
                    dve.wait_ge(s_["e_ps"], g + 1)
                    dve.tensor_scalar(esc[:], ps[4][:, 0:G], b3c[:, 0:1], 0.0, ALU.add, ALU.max).then_inc(s_["esc_ok"], 1)
                    dve.wait_ge(s_["esc_ok"], g + 1)
                    dve.tensor_tensor(gv[:, :, 0:D], gv[:, :, 0:D],
                                      esc[:].rearrange("p (k u) -> p k u", u=1).to_broadcast([P, G, D]), ALU.mult).then_inc(s_["ge_ok"], 1)
                    accumulate(EDGE, i, r, X)
                    dve.sem_inc(s_["out_ok"], 1)

            turns(dve, NG // R, edges)
            dve.sem_inc(s_["pass_ok"], 1)


_INS = ['x', 'src', 'dst', 'edge_attr_8', 'edge_type_16', 'edge_weight', 'L0_gnn_basis_msg_wt', 'L0_gnn_basis_msg_bias',
        'L0_gnn_basis_self_wt', 'L0_gnn_basis_self_bias', 'L0_gnn_lin_comb', 'L1_gnn_weight', 'L3_gnn_W_src', 'L3_gnn_b_src',
        'L3_gnn_W_tgt', 'L3_gnn_b_tgt', 'L3_gnn_W_edge', 'L3_gnn_b_edge', 'L3_gnn_W1', 'L3_gnn_b1', 'L3_gnn_W2', 'L3_gnn_b2',
        'L3_gnn_W3', 'L3_gnn_b3']


def kernel(**inputs):
    import numpy as _np
    import concourse.bacc as _bacc
    from concourse import mybir as _mybir
    from concourse.bass_utils import run_bass_kernel_spmd as _run

    nc = _bacc.Bacc("TRN2", target_bir_lowering=False, num_devices=1)
    arrays, args = {}, []
    for name in _INS:
        a = _np.ascontiguousarray(inputs[name])
        arrays[f"in_{name}_dram"] = a
        args.append(nc.dram_tensor(f"in_{name}_dram", a.shape, _mybir.dt.from_np(a.dtype), kind="ExternalInput").ap())
    o = nc.dram_tensor("out_0_dram", inputs['x'].shape, _mybir.dt.float32, kind="ExternalOutput").ap()
    gnn_kernel(nc, *args, o)
    r = _run(nc, [arrays], core_ids=[0])
    return r.results[0]["out_0_dram"]
```

```python
from contextlib import ExitStack

import concourse.bass as bass
from concourse import mybir

F32 = mybir.dt.float32
I32 = mybir.dt.int32
I16 = mybir.dt.int16
ALU = mybir.AluOpType
ACT = mybir.ActivationFunctionType
AX = mybir.AxisListType

P = 128
LN_EPS = 1e-5
L2_EPS = 1e-12
NEG_SLOPE = 0.01
G = 8
R = 4


def gnn_kernel(nc, x, src, dst, edge_attr, etype, eweight, msg_wt, msg_b, self_wt, self_b, lin, rel_w,
               W_src, b_src, W_tgt, b_tgt, W_edge, b_edge, W1, b1, W2, b2, W3, b3, out):
    N, D = x.shape
    E = src.shape[0]
    EA = edge_attr.shape[1]
    NREL = rel_w.shape[0]
    NBASE = msg_wt.shape[2]
    H2 = W2.shape[0]
    NODE_BLOCKS = -(-N // P)
    BG = 4
    NJ = -(-NODE_BLOCKS // BG)
    NB = NJ * BG
    NP = NB * P
    TILES = -(-E // P)
    assert NJ % 2 == 1 and NJ >= 5
    NC = -(-(TILES + NODE_BLOCKS - 1) // P)
    STEPS = NC * P
    assert STEPS % (G * R) == 0 and D == 64 and G * EA == 64 and H2 == 32
    NG = STEPS // G
    PAD_DST = NODE_BLOCKS * P - 1
    assert PAD_DST >= N
    DA = D + 1
    NH = 3
    assert NB * P + P < 2 ** 15
    NT = G
    ACC_ROWS = NP + P
    EDGE = 2

    with ExitStack() as ctx:
        def sb(name, shape, dt=F32):
            return ctx.enter_context(nc.sbuf_tensor(name, shape, dt))

        def sem(name):
            return ctx.enter_context(nc.semaphore(name))

        def dram(name, shape, dt=F32):
            return nc.dram_tensor(name, shape, dt).ap()

        rec_d = dram("rec_d", (STEPS, 4, P), I32)
        attr_d = dram("attr_d", (STEPS, P * EA))
        start_d = dram("start_d", (STEPS,))
        q_d = dram("q_d", (STEPS, 1))
        blk_d = dram("blk_d", (STEPS,), I32)
        rel_d = dram("rel_d", (STEPS, P), I16)
        attr_s = dram("attr_s", (NG, P, G * EA))
        tab0 = dram("tab0", (NP, D))
        tab1 = dram("tab1", (NP, NREL * D))
        acc_d = [[dram(f"acc_d{m}_{t}", (ACC_ROWS, D)) for t in range(NT)] for m in range(NH)]
        src_d = dram("src_d", (STEPS, P), I16)
        tab3 = dram("tab3", (NP, 2 * D))

        X = sb("X", [P, NB * D])
        H = sb("H", [P, NB * DA])
        TMP = sb("TMP", [P, NB * D])
        AG = sb("AG", [P, NB * D])
        Xv = X[:].rearrange("p (b f) -> p b f", f=D)
        Hv = H[:].rearrange("p (b f) -> p b f", f=DA)[:, :, 0:D]
        Hone = H[:].rearrange("p (b f) -> p b f", f=DA)[:, :, D:DA]
        TMPv = TMP[:].rearrange("p (b f) -> p b f", f=D)
        AGv = AG[:].rearrange("p (b f) -> p b f", f=D)
        s1 = sb("s1", [P, NB])
        s2 = sb("s2", [P, NB])
        s3 = sb("s3", [P, NB])
        srcT = sb("srcT", [P, STEPS], I32)
        rowT = sb("rowT", [P, STEPS], I32)
        relT = sb("relT", [P, STEPS])
        wT = sb("wT", [P, STEPS])
        blkR = sb("blkR", [1, STEPS], I32)
        idx = sb("idx", [P, R, G], I32)
        gat = sb("gat", [P, R, G * 2 * D])
        S = sb("S", [P, 2, G, P])
        ST = sb("ST", [P, 2, G, P])
        attrG = sb("attrG", [P, R, G * EA])
        attrT = sb("attrT", [G * EA, 2, P])
        pre = sb("pre", [P, 2, G * D])
        h1 = sb("h1", [P, G * D])
        h1r = sb("h1r", [P, G * D])
        h2 = sb("h2", [2 * H2, G * D])
        h2r = sb("h2r", [2 * H2, G * D])
        esc = sb("esc", [P, G])
        dups = sb("dups", [P, G])
        away = sb("away", [P, G])
        junkP = sb("junkP", [P, 1])
        TO = sb("TO", [P, BG * NREL * D])
        HS = sb("HS", [P, 2, BG * DA])
        HT = sb("HT", [DA, 2, BG * P])
        raw = TO[:, 0:R * 2 * G * P // 2].bitcast(I16).rearrange("p (r t e) -> p r t e", r=R, t=2)
        iotaN = sb("iotaN", [P, P])
        iotaI = sb("iotaI", [P, P], I32)
        iotaP = sb("iotaP", [P, 1])
        iotaPi = sb("iotaPi", [P, 1], I32)
        ident = sb("ident", [P, P])
        stepN = sb("stepN", [P, NC])
        lower = sb("lower", [P, P])
        linB = sb("linB", [DA, NBASE])
        W0 = sb("W0", [DA, 2 * D])
        WR = sb("WR", [D, NREL * D])
        As = sb("As", [D, DA])
        At = sb("At", [D, DA])
        Ae = sb("Ae", [D, EA])
        be = sb("be", [D, 1])
        W1n = sb("W1n", [D, 3 * D])
        W1t = sb("W1t", [D, 4 * D])
        W2n = sb("W2n", [2 * H2, P])
        W3n = sb("W3n", [2, 2 * H2])
        W2t = sb("W2t", [P, 2 * H2])
        W3t = sb("W3t", [2 * H2, 2])
        W4 = sb("W4", [DA, 4 * D])
        We = sb("We", [EA, D])
        Web = sb("Web", [G * EA, G, D])
        b1c = sb("b1c", [P, 1])
        b1s = sb("b1s", [P, 1])
        b2c = sb("b2c", [2 * H2, 1])
        b3c = sb("b3c", [P, 1])
        dstI = TO[:, 0:STEPS].bitcast(I32)
        srcI = TO[:, STEPS:2 * STEPS].bitcast(I32)
        wI = AG[:, 0:STEPS].bitcast(I32)
        tyI = AG[:, STEPS:2 * STEPS].bitcast(I32)
        startB = H[:, 0:STEPS]
        leq = TMP[:, 0:STEPS]
        blo = sb("blo", [P, NC])
        cnt = sb("cnt", [P, NC])
        edgeB = sb("edgeB", [P, 2, NC], I32)
        start = sb("start", [P, NC])
        q = sb("q", [P, NC])
        tot = sb("tot", [P, 1])
        tile_i = sb("tile_i", [P, NC], I32)
        tcol = sb("tcol", [P, 1], I32)
        rg = gat[:, 0, 0:4 * P].bitcast(I32)
        eg = gat[:, 1, :]
        qg = sb("qg", [P, 1])
        nblk = sb("nblk", [P, 1])
        blkf = sb("blkf", [P, 1])
        blki = sb("blki", [P, 1], I32)
        stepc = sb("stepc", [P, 1])
        fld = gat[:, 2, 0:4 * P]
        fld16 = gat[:, 2, 4 * P:5 * P].bitcast(I16).rearrange("p (t e) -> p t e", t=2)
        eo = gat[:, 3, :]

        ps = [ctx.enter_context(nc.psum_tensor(f"ps{i}", [P, 512], F32)) for i in range(8)]

        SEMS = """src_rows gathers_begun turns_begun zero_ok pool_const const_ok edges_in lin_in w_in w0_ok rel_in mlp_in mlp_const mlp_T mlp_Tc
            mlp_mm mlp_c web_in rec_out attr_out attr_tail q_out start_in base_mm tcol_ok stair_g stair_f
            stair_T stair_e stair_out tiles_ok blk_in stair_done dve stair_d x_in ln_var ln_std ln_ok hs_ok
            hT_ps ht_ok proj_ps proj_mv proj_act nrm_in nrm_out tabs_zero hop_go hop_ST hop_M msg_ps msg_ok sum_ps rows_ok dup_ok sum_mv idx_ok mm_ok S_ok acc_ok
            esc_ok ST_ok aT_ps aT_ok pre_ps pre_ok h1_ps h1_sb h1_ok h2_ps h2_sb h2_ok e_ps ge_ok pass_ok out_in
            """.split()
        sems = {n: sem(n) for n in SEMS}
        gather_ok = [sem(f"gather_ok{r}") for r in range(R)]

        scat_ok = [sem(f"scat_ok{h}") for h in range(2)]
        rows_in = [sem(f"rows_in{r}") for r in range(R)]
        attr_in = [sem(f"attr_in{r}") for r in range(R)]
        tab_out = [sem(f"tab_out{h}") for h in range(2)]
        sum_in = [sem(f"sum_in{h}") for h in range(2)]

        block = ctx.enter_context(nc.Block())
        s_ = sems
        FULL = E // STEPS
        REST = E - FULL * STEPS
        NFULL = N // P
        PZ = next(u for u in range(1, 64) if ACC_ROWS % (P * u) == 0 and ACC_ROWS // (P * u) <= G)
        NREST = N - NFULL * P
        tail = STEPS * P * EA - E * EA
        assert tail % 16 == 0 and NB * D * 16 < tail <= 2 * NB * D * 16 and (E * EA) % 880 == 0

        def wait(eng, semaphore, value):
            if not isinstance(value, int) or value > 0:
                eng.wait_ge(semaphore, value)

        def turns(eng, n, body):
            body(0)
            with eng.Fori(1, n - 1) as i:
                body(i)
            body(n - 1)

        @block.sync
        def _(sp):
            sp.wait_ge(s_["zero_ok"], 1)
            for dstb, a in ((dstI, dst), (srcI, src), (wI, eweight.bitcast(I32)), (tyI, etype)):
                sp.dma_start(dstb[0:FULL, :], a[0:FULL * STEPS].rearrange("(p j) -> p j", j=STEPS)).then_inc(s_["edges_in"], 16)
                sp.dma_start(dstb[FULL:FULL + 1, 0:REST], a[FULL * STEPS:E].rearrange("(p j) -> p j", p=1)).then_inc(s_["edges_in"], 16)
            flat = attr_d.rearrange("t j -> (t j)")
            sp.dma_start(flat[0:E * EA].rearrange("(a b) -> a b", a=880),
                         edge_attr.rearrange("e a -> (e a)").rearrange("(a b) -> a b", a=880)).then_inc(s_["attr_out"], 16)
            for a0, a1 in ((0, NB * D * 16), (NB * D * 16, tail)):
                sp.dma_start(flat[E * EA + a0:E * EA + a1].rearrange("(a b) -> a b", a=16),
                             X[0:16, 0:(a1 - a0) // 16]).then_inc(s_["attr_tail"], 16)
            for half, (wt, bias) in enumerate(((msg_wt, msg_b), (self_wt, self_b))):
                wv = srcT if half == 0 else rowT
                sp.dma_start(wv[0:D, 0:D * NBASE].bitcast(F32), wt.rearrange("i o b -> i (o b)")).then_inc(s_["w_in"], 16)
                sp.dma_start(wv[D:DA, 0:D * NBASE].bitcast(F32), bias.rearrange("(u o) b -> u (o b)", u=1)).then_inc(s_["w_in"], 16)
            sp.dma_start(linB[:], lin.to_broadcast([DA, NBASE])).then_inc(s_["w_in"], 16)
            sp.dma_start(WR[:].rearrange("i (r o) -> i r o", r=NREL), rel_w.rearrange("r i o -> i r o")).then_inc(s_["rel_in"], 16)
            col = lambda a: a.rearrange("(p u) -> p u", u=1)
            sp.wait_ge(s_["zero_ok"], 2)
            for o, i in ((As[:, 0:D], W_src), (As[:, D:DA], col(b_src)), (At[:, 0:D], W_tgt), (At[:, D:DA], col(b_tgt)),
                         (Ae[:], W_edge), (be[:], col(b_edge)), (W1n[:], W1),
                         (W2n[0:H2, 0:D], W2), (W2n[H2:2 * H2, D:P], W2),
                         (W3n[0:1, 0:H2], W3), (W3n[1:2, H2:2 * H2], W3),
                         (b1s[0:D, :], col(b1)), (b1s[D:P, :], col(b1)), (b2c[0:H2, :], col(b2)), (b2c[H2:2 * H2, :], col(b2)),
                         (b3c[:], b3.rearrange("(u v) -> u v", u=1).to_broadcast([P, 1]))):
                sp.dma_start(o, i).then_inc(s_["mlp_in"], 16)
            sp.wait_ge(s_["src_rows"], 1)
            for f, b in enumerate((srcI, dstI, wI, tyI)):
                sp.dma_start(rec_d.rearrange("(p c) f j -> p c f j", c=NC)[:, :, f, :],
                             b.rearrange("p (c j) -> p c j", j=P)).then_inc(s_["rec_out"], 16)
            sp.wait_ge(s_["tiles_ok"], 1)
            sp.dma_start(start_d.rearrange("(p c) -> p c", c=NC), start[:]).then_inc(s_["q_out"], 16)
            sp.dma_start(q_d.rearrange("(p c) u -> p (c u)", c=NC), q[:]).then_inc(s_["q_out"], 16)
            sp.wait_ge(s_["q_out"], 32)
            sp.dma_start(startB, start_d.rearrange("(u s) -> u s", u=1).to_broadcast([P, STEPS])).then_inc(s_["start_in"], 16)
            with sp.Fori(0, NC) as c:
                sp.wait_ge(s_["stair_f"], c + 1)
                sp.dma_start(rel_d[bass.ds(c * P, P), :], fld16[:, 1, :]).then_inc(s_["stair_out"], 16)
                sp.dma_start(src_d[bass.ds(c * P, P), :], fld16[:, 0, :]).then_inc(s_["stair_out"], 16)
                sp.dma_start(blk_d[bass.ds(c * P, P)].rearrange("(p u) -> p u", u=1), blki[:]).then_inc(s_["stair_out"], 16)
                sp.wait_ge(s_["stair_e"], c + 1)
                sp.dma_start(attr_s[bass.ds(c * (P // G), P // G), :, :].rearrange("g p m -> p g m"),
                             eo.rearrange("p (g m) -> p g m", m=G * EA)).then_inc(s_["stair_out"], 16)
            sp.wait_ge(s_["stair_out"], 64 * NC)
            sp.dma_start(blkR[:], blk_d.rearrange("(u s) -> u s", u=1)).then_inc(s_["blk_in"], 16)
            sp.wait_ge(s_["attr_tail"], 32)
            sp.dma_start(Xv[:, 0:NFULL, :], x[0:NFULL * P, :].rearrange("(b p) f -> p b f", p=P)).then_inc(s_["x_in"], 16)
            sp.dma_start(Xv[0:NREST, NFULL, :], x[NFULL * P:N, :]).then_inc(s_["x_in"], 16)
            for k in range(G):
                if k == 0:
                    sp.wait_ge(s_["mlp_c"], 3)
                sp.dma_start(Web[k * EA:(k + 1) * EA, k, :], We[:]).then_inc(s_["web_in"], 16)

            def tables(n, tab, width):
                hb = BG // 2

                def group(j):
                    for h in range(2):
                        sp.wait_ge(s_["proj_mv"], (n * NJ + j) * BG + (h + 1) * hb)
                        if not isinstance(j, int):
                            sp.sem_inc(s_["turns_begun"], 1)
                        if width > 512:
                            sp.wait_ge(s_["proj_act"], j * BG + (h + 1) * hb)
                        sp.dma_start(tab.rearrange("(p b) f -> p b f", p=P)[:, bass.ds(j * BG + h * hb, hb), :],
                                     TO[:, h * hb * width:(h + 1) * hb * width].rearrange("p (b f) -> p b f", f=width)).then_inc(tab_out[h], 16)

                turns(sp, NJ, group)

            tables(0, tab0, D)
            sp.wait_ge(s_["zero_ok"], 2)
            for m in range(NH):
                for t in range(NT):
                    sp.dma_start(acc_d[m][t].rearrange("(p u b) f -> p u (b f)", p=P, u=PZ),
                                 pre[:, 0, 0:ACC_ROWS * D // (P * PZ)].rearrange("p (v w) -> p v w", v=1).to_broadcast([P, PZ, ACC_ROWS * D // (P * PZ)])).then_inc(s_["tabs_zero"], 16)
            tables(1, tab1, NREL * D)
            for m in range(NH):
                sp.wait_ge(s_["hop_go"], 2 * m + 1)

                def rows(i):
                    for r in range(R):
                        g = i * R + r
                        wait(sp, s_["hop_M"], m * NG + g - R + 1)
                        for t, tab in enumerate((rel_d, src_d)):
                            sp.dma_start(raw[:, r, t, :], tab[bass.ds(g * G, G), :].rearrange("(u k) e -> u (k e)", u=1)
                                         .to_broadcast([P, G * P])).then_inc(rows_in[r], 16)

                turns(sp, NG // R, rows)
                for h in range(2):
                    sp.wait_ge(scat_ok[h], (m + 1) * NG * 16 * (G // 2))
                sp.wait_ge(s_["hop_go"], 2 * m + 2)
                for t in range(NT):
                    if t >= 2:
                        sp.wait_ge(s_["sum_mv"], m * NT + t - 1)
                    sp.dma_start((TMPv, TO[:, 0:NB * D].rearrange("p (b f) -> p b f", f=D))[t % 2],
                                 acc_d[m][t][0:NP, :].rearrange("(p b) f -> p b f", p=P)).then_inc(sum_in[t % 2], 16)
            tables(2, tab3, 2 * D)
            sp.wait_ge(s_["proj_mv"], 3 * NJ * BG)

            def edge_rows(i):
                for r in range(R):
                    g = i * R + r
                    wait(sp, s_["ST_ok"], g - R + 1)
                    sp.dma_start(raw[:, r, 0, :], rel_d[bass.ds(g * G, G), :].rearrange("(u k) e -> u (k e)", u=1)
                                 .to_broadcast([P, G * P])).then_inc(rows_in[r], 16)
                    wait(sp, s_["aT_ps"], g - R + 1)
                    sp.dma_start(attrG[:, r, :], attr_s[bass.ds(g, 1), :, :].rearrange("g p m -> (g p) m")).then_inc(attr_in[r], 16)

            for h in range(2):
                sp.wait_ge(tab_out[h], 48 * NJ)
            turns(sp, NG // R, edge_rows)
            sp.wait_ge(s_["pass_ok"], 1)
            sp.dma_start(out[0:NFULL * P, :].rearrange("(b p) f -> p b f", p=P), Xv[:, 0:NFULL, :]).then_inc(s_["out_in"], 16)
            sp.dma_start(out[NFULL * P:N, :], Xv[0:NREST, NFULL, :]).then_inc(s_["out_in"], 16)
            sp.wait_ge(s_["out_in"], 32)

        @block.gpsimd
        def _(pool):
            pool.iota(iotaI[:], [[1, P]], base=0, channel_multiplier=0).then_inc(s_["pool_const"], 1)
            pool.iota(iotaPi[:], [[0, 1]], base=0, channel_multiplier=1).then_inc(s_["pool_const"], 1)
            pool.memset(ident[:], 0.0).then_inc(s_["pool_const"], 1)
            pool.memset(lower[:], 1.0).then_inc(s_["pool_const"], 1)
            pool.wait_ge(s_["pool_const"], 4)
            pool.affine_select(out=ident[:], in_=ident[:], compare_op=ALU.not_equal, fill=1.0, base=0,
                               pattern=[[-1, P]], channel_multiplier=1).then_inc(s_["pool_const"], 1)
            pool.affine_select(out=lower[:], in_=lower[:], compare_op=ALU.is_gt, fill=0.0, base=0,
                               pattern=[[1, P]], channel_multiplier=-1).then_inc(s_["pool_const"], 1)
            pool.iota(tile_i[:], [[P, NC]], base=0, channel_multiplier=1).then_inc(s_["pool_const"], 1)
            pool.wait_ge(s_["rec_out"], 64)
            pool.wait_ge(s_["attr_out"], 16)
            pool.wait_ge(s_["attr_tail"], 32)
            with pool.Fori(0, NC) as c:
                pool.wait_ge(s_["tcol_ok"], c + 1)
                pool.sem_inc(s_["gathers_begun"], 1)
                off = bass.IndirectOffsetOnAxis(ap=tcol[:], axis=0)
                pool.indirect_dma_start(rg, None, rec_d.rearrange("t f j -> t (f j)"), off).then_inc(s_["stair_g"], 16)
                pool.indirect_dma_start(eg, None, attr_d, off).then_inc(s_["stair_g"], 16)
                pool.indirect_dma_start(qg[:], None, q_d, off).then_inc(s_["stair_g"], 16)

            def gathers(n, table, width):
                with pool.Fori(0, NG // R) as i:
                    for r in range(R):
                        pool.wait_ge(s_["idx_ok"], i * R + n * NG + r + 1)
                        pool.sem_inc(s_["gathers_begun"], 1)
                        for k in range(G):
                            pool.indirect_dma_start(gat[:, r, k * width:(k + 1) * width], None, table,
                                                    bass.IndirectOffsetOnAxis(ap=idx[:, r, k:k + 1], axis=0)).then_inc(gather_ok[r], 16)

            for h in range(2):
                pool.wait_ge(tab_out[h], 16 * NJ)
            gathers(0, tab0, D)
            for h in range(2):
                pool.wait_ge(tab_out[h], 32 * NJ)
            gathers(1, tab1.rearrange("n (r f) -> (n r) f", f=D), D)
            pool.wait_ge(s_["tabs_zero"], 16 * NH * NT)
            for m in range(NH):
                def scatters(i):
                    for r in range(R):
                        g = i * R + r
                        pool.wait_ge(s_["rows_ok"], m * NG + g + 1)
                        if not isinstance(g, int):
                            pool.sem_inc(s_["gathers_begun"], 1)
                        for k in range(G):
                            if k % (G // 2) == 0:
                                h = k // (G // 2)
                                wait(pool, scat_ok[h], (m * NG + g) * 16 * (G // 2))
                                if not isinstance(g, int):
                                    pool.sem_inc(s_["gathers_begun"], 1)
                            pool.indirect_dma_start(acc_d[m][k], bass.IndirectOffsetOnAxis(ap=idx[:, r, k:k + 1], axis=0),
                                                    gat[:, r, k * D:(k + 1) * D], None, compute_op=ALU.add).then_inc(scat_ok[k // (G // 2)], 16)

                turns(pool, NG // R, scatters)
            for h in range(2):
                pool.wait_ge(tab_out[h], 48 * NJ)
            gathers(EDGE, tab3, 2 * D)

        @block.scalar
        def _(act):
            act.wait_ge(s_["mlp_T"], 1)
            act.copy(W1t[:], ps[0][0:D, 0:4 * D]).then_inc(s_["mlp_Tc"], 1)
            act.copy(W2t[:], ps[1][:, 0:2 * H2])
            act.copy(W3t[:], ps[1][0:2 * H2, P:P + 2]).then_inc(s_["mlp_Tc"], 2)
            act.wait_ge(s_["mlp_mm"], 1)
            act.wait_ge(s_["zero_ok"], 2)
            act.copy(W4[:], ps[2][0:DA, 0:4 * D]).then_inc(s_["mlp_c"], 1)
            act.activation(b1c[:], ps[3][:, 0:1], ACT.Identity, bias=b1s[:, 0:1]).then_inc(s_["mlp_c"], 1)
            act.copy(We[:], ps[3][0:EA, D:2 * D]).then_inc(s_["mlp_c"], 1)
            def attributes(c):
                act.wait_ge(s_["stair_T"], c + 1)
                wait(act, s_["stair_out"], c * 64)
                for hb in range(2):
                    o = eo.rearrange("p (s a) -> p a s", a=EA)[:, 4 * hb:4 * hb + 4, :]
                    ins = act.copy(o, ps[5 + hb][:].rearrange("p (a s) -> p a s", a=4))
                ins.then_inc(s_["stair_e"], 1)

            turns(act, NC, attributes)

            def std(n):
                act.wait_ge(s_["ln_var"], n)
                act.activation(s3[:], s2[:], ACT.Sqrt).then_inc(s_["ln_std"], 1)

            def turn(n):
                def stage(j, q):
                    wait(act, s_["hT_ps"], n * NJ + j - 1)
                    act.copy(HS[:, q, :], H[:, bass.ds(j * (BG * DA), BG * DA)]).then_inc(s_["hs_ok"], 1)
                    act.wait_ge(s_["hT_ps"], n * NJ + j + 1)
                    wait(act, s_["proj_ps"], (n * NJ + j - 1) * BG)
                    act.copy(HT[:, q, :], ps[q][0:DA, :]).then_inc(s_["ht_ok"], 1)

                def move(j):
                    for b in range(BG):
                        if b % 2 == 0:
                            wait(act, tab_out[b // 2], (n * NJ + j) * 16)
                        act.wait_ge(s_["proj_ps"], (n * NJ + j) * BG + b + 1)
                        act.copy(TO[:, b * NREL * D + 512:(b + 1) * NREL * D], ps[3 + 2 * (b % 2)][:]).then_inc(s_["proj_act"], 1)

                stage(0, 0)
                for j in (0, 1):
                    stage(j + 1, (j + 1) % 2)
                    if n == 1:
                        move(j)
                with act.Fori(1, (NJ - 1) // 2) as i:
                    for h in range(2):
                        stage(i * 2 + (h + 1), 1 - h)
                        if n == 1:
                            move(i * 2 + h)
                if n == 1:
                    move(NJ - 1)

            def indices(n, table):
                with act.Fori(0, NG // R) as i:
                    for r in range(R):
                        act.wait_ge(s_["mm_ok"], i * R + n * NG + r + 1)
                        act.copy(idx[:, r, :], table[:, bass.ds(i * (R * G) + r * G, G)]).then_inc(s_["idx_ok"], 1)

            std(1)
            act.wait_ge(s_["ln_ok"], 1)
            turn(0)
            act.wait_ge(s_["stair_done"], 1)
            indices(0, srcT)
            act.wait_ge(s_["nrm_in"], 1)
            act.activation(s3[:], s2[:], ACT.Sqrt).then_inc(s_["nrm_out"], 1)
            std(2)
            act.wait_ge(s_["ln_ok"], 2)
            turn(1)
            indices(1, rowT)
            std(3)
            for m in range(NH):
                def out_rows(i):
                    for r in range(R):
                        g = i * R + r
                        act.wait_ge(s_["sum_ps"], m * NG + g + 1)
                        for h in range(2):
                            wait(act, scat_ok[h], (m * NG + g - R + 1) * 16 * (G // 2))
                        act.copy(idx[:, r, :], rowT[:, bass.ds(g * G, G)])
                        act.copy(gat[:, r, 0:G * D], ps[2 + r % 2][:]).then_inc(s_["rows_ok"], 1)

                turns(act, NG // R, out_rows)
            std(4)
            act.wait_ge(s_["ln_ok"], 4)
            turn(2)
            for r in range(R):
                act.wait_ge(s_["mm_ok"], EDGE * NG + r + 1)
                act.copy(idx[:, r, :], srcT[:, r * G:(r + 1) * G]).then_inc(s_["idx_ok"], 1)

            def attr_turn(g, h):
                act.wait_ge(s_["aT_ps"], g + 1)
                act.copy(attrT[:, h, :], ps[5 * h][0:G * EA, 0:P]).then_inc(s_["aT_ok"], 1)

            def edges(i):
                for r in range(R):
                    g = i * R + r
                    if not (isinstance(g, int) and g >= NG - 2):
                        attr_turn(g + 2, r % 2)
                    act.wait_ge(s_["h1_ps"], g + 1)
                    act.activation(h1[:], ps[2][:], ACT.Identity, bias=b1c[:, 0:1]).then_inc(s_["h1_sb"], 1)
                    act.wait_ge(s_["h2_ps"], g + 1)
                    act.activation(h2[:], ps[3][0:2 * H2, :], ACT.Identity, bias=b2c[:, 0:1]).then_inc(s_["h2_sb"], 1)
                    q = (r - 1) % R
                    if isinstance(g, int) and (g == 0 or g - 1 + R >= NG):
                        continue
                    act.wait_ge(s_["mm_ok"], g + (EDGE * NG + R))
                    act.copy(idx[:, q, :], srcT[:, bass.ds((g + (R - 1)) * G, G)]).then_inc(s_["idx_ok"], 1)

            attr_turn(0, 0)
            attr_turn(1, 1)
            turns(act, NG // R, edges)

        @block.tensor
        def _(pe):
            pe.wait_ge(s_["const_ok"], 1)
            pe.sem_inc(s_["mm_ok"], R)
            pe.wait_ge(s_["mlp_in"], 16 * 16)
            for k in range(4):
                pe.transpose(ps[0][0:D, k * D:(k + 1) * D], W1n[:, min(k, 2) * D:min(k, 2) * D + D], ident[0:D, 0:D])
            pe.transpose(ps[1][:, 0:2 * H2], W2n[:], ident[0:2 * H2, 0:2 * H2])
            pe.transpose(ps[1][0:2 * H2, P:P + 2], W3n[:], ident[0:2, 0:2])
            pe.transpose(ps[2][0:DA, 0:D], As[:], ident[0:D, 0:D])
            pe.transpose(ps[2][0:DA, 2 * D:3 * D], At[:], ident[0:D, 0:D]).then_inc(s_["mlp_T"], 1)
            pe.wait_ge(s_["mlp_Tc"], 3)
            pe.matmul(ps[2][0:DA, D:2 * D], As[:], W1t[:, 0:D], start=True, stop=True)
            pe.matmul(ps[2][0:DA, 3 * D:4 * D], At[:], W1t[:, D:2 * D], start=True, stop=True)
            pe.matmul(ps[3][:, 0:1], W1t[:, 2 * D:4 * D], be[:], start=True, stop=True)
            pe.matmul(ps[3][0:EA, D:2 * D], Ae[:], W1t[:, 2 * D:3 * D], start=True, stop=True).then_inc(s_["mlp_mm"], 1)
            pe.wait_ge(s_["base_mm"], 1)
            pe.matmul(ps[4][:, 0:1], lower[:], tot[:], start=True, stop=True).then_inc(s_["base_mm"], 1)
            def columns(c):
                pe.wait_ge(s_["stair_f"], c + 1)
                for f in range(4):
                    src_ap = fld[:, f * P:(f + 1) * P] if f != 2 else rg[:, 2 * P:3 * P].bitcast(F32)
                    pe.transpose(ps[4][:, f * P:(f + 1) * P], src_ap, ident[:])
                wait(pe, s_["stair_e"], c)
                for a in range(EA):
                    ins = pe.transpose(ps[5 + a // 4][:, (a % 4) * P:(a % 4 + 1) * P],
                                       eg.rearrange("p (e a) -> p a e", a=EA)[:, a, :], ident[:])
                ins.then_inc(s_["stair_T"], 1)

            turns(pe, NC, columns)

            def project(n, w, width, k):
                def turn(j, q):
                    pe.wait_ge(s_["hs_ok"], n * NJ + j + 1)
                    wait(pe, s_["ht_ok"], n * NJ + j - 1)
                    for b in range(BG):
                        ins = pe.transpose(ps[q][0:DA, b * P:(b + 1) * P], HS[:, q, b * DA:(b + 1) * DA], ident[:])
                    ins.then_inc(s_["hT_ps"], 1)

                def products(j, q):
                    pe.wait_ge(s_["ht_ok"], n * NJ + j + 1)
                    for b in range(BG):
                        bank = 2 + 2 * (b % 2)
                        wait(pe, s_["proj_mv"], (n * NJ + j) * BG + b - 1)
                        if width > 512:
                            wait(pe, s_["proj_act"], j * BG + b - 1)
                        for w0 in range(0, width, 512):
                            c = min(512, width - w0)
                            ins = pe.matmul(ps[bank + w0 // 512][:, 0:c], HT[0:k, q, b * P:(b + 1) * P], w[0:k, w0:w0 + c],
                                            start=True, stop=True)
                        ins.then_inc(s_["proj_ps"], 1)

                turn(0, 0)
                for j in (0, 1):
                    turn(j + 1, 1 - j)
                    products(j, j)
                with pe.Fori(1, (NJ - 1) // 2) as i:
                    for h in range(2):
                        turn(i * 2 + (h + 1), 1 - h)
                        products(i * 2 + h, h)
                products(NJ - 1, 0)

            def segment(n):
                def groups(i):
                    for r in range(R):
                        pe.wait_ge(gather_ok[r], i * (16 * G) + (n * (NG // R) + 1) * 16 * G)
                        pe.wait_ge(s_["S_ok"], i * R + n * NG + r + 1)
                        wait(pe, s_["acc_ok"], (i * R + n * NG + r - 1) * G)
                        for k in range(G):
                            ins = pe.matmul(ps[6 + r % 2][:, k * D:(k + 1) * D], S[:, r % 2, k, :], gat[:, r, k * D:(k + 1) * D],
                                            start=True, stop=True)
                        ins.then_inc(s_["mm_ok"], 1)

                turns(pe, NG // R, groups)

            pe.wait_ge(s_["mlp_c"], 3)
            pe.wait_ge(s_["stair_e"], NC)
            pe.wait_ge(s_["stair_done"], 1)
            pe.wait_ge(s_["w0_ok"], 1)
            project(0, W0, 2 * D, DA)
            segment(0)
            pe.wait_ge(s_["rel_in"], 16)
            project(1, WR, NREL * D, D)
            segment(1)
            regs = [pe.alloc_register(f"pe_blk{k}") for k in range(G)]

            def spread(bank, g, h, attributes):
                pe.reg_load(regs, blkR[0:1, bass.ds(g * G, G)])
                cols = [pe.snap(x_, min_val=0, max_val=(NODE_BLOCKS - 1) * D) for x_ in regs]
                if attributes:
                    pe.matmul(ps[bank][:], attrT[:, h, :], Web[:].rearrange("p k f -> p (k f)"), start=True, stop=True)
                for k in range(G):
                    ins = pe.matmul(ps[bank][:, k * D:(k + 1) * D], ST[:, h, k, :], AG[:, bass.ds(cols[k], D)],
                                    start=not attributes, stop=True, skip_group_check=attributes)
                return ins

            for m in range(NH):
                def spread_next(g, h):
                    pe.wait_ge(s_["hop_ST"], m * NG + g + 1)
                    spread(h, g, h, False).then_inc(s_["msg_ps"], 1)

                def hops(i):
                    for r in range(R):
                        g, h = i * R + r, r % 2
                        if not (isinstance(g, int) and g == NG - 1):
                            spread_next(g + 1, 1 - h)
                        pe.wait_ge(s_["msg_ok"], m * NG + g + 1)
                        wait(pe, s_["rows_ok"], m * NG + g - 1)
                        for k in range(G):
                            ins = pe.matmul(ps[2 + h][:, k * D:(k + 1) * D], S[:, h, k, :], pre[:, h, k * D:(k + 1) * D],
                                            start=True, stop=True)
                        ins.then_inc(s_["sum_ps"], 1)

                spread_next(0, 0)
                turns(pe, NG // R, hops)
            project(2, W4, 4 * D, DA)
            pe.wait_ge(s_["web_in"], 16 * G)

            def attr_turn(g, i, r):
                pe.wait_ge(attr_in[r], (i + 1) * 16)
                if not isinstance(g, int):
                    pe.sem_inc(s_["turns_begun"], 1)
                pe.transpose(ps[5 * (r % 2)][0:G * EA, 0:P], attrG[:, r, :], ident[:]).then_inc(s_["aT_ps"], 1)

            def first_layer(g, h):
                pe.wait_ge(s_["ST_ok"], g + 1)
                pe.wait_ge(s_["aT_ok"], g + 1)
                spread(1, g, h, True).then_inc(s_["pre_ps"], 1)

            def segment_edges(g, r):
                h = r % 2
                pe.wait_ge(s_["ge_ok"], g + 1)
                pe.wait_ge(s_["acc_ok"], (EDGE * NG + g - 1) * G)
                for k in range(G):
                    ins = pe.matmul(ps[6 + h][:, k * D:(k + 1) * D], S[:, h, k, :], gat[:, r, k * 2 * D:k * 2 * D + D],
                                    start=True, stop=True)
                ins.then_inc(s_["mm_ok"], 1)

            def edges(i):
                for r in range(R):
                    g = i * R + r
                    last = isinstance(g, int) and g == NG - 1
                    if not (isinstance(g, int) and g >= NG - 2):
                        attr_turn(g + 2, i if r < R - 2 else i + 1, (r + 2) % R)
                    pe.wait_ge(s_["pre_ok"], g + 1)
                    for k in range(G // 2):
                        ins = pe.transpose(ps[2][:, k * P:(k + 1) * P], pre[:, 0, k * P:(k + 1) * P], ident[:])
                    ins.then_inc(s_["h1_ps"], 1)
                    if not last:
                        first_layer(g + 1, (r + 1) % 2)
                    pe.wait_ge(s_["h1_ok"], g + 1)
                    pe.matmul(ps[3][0:2 * H2, :], W2t[:], h1r[:], start=True, stop=True).then_inc(s_["h2_ps"], 1)
                    if not (isinstance(g, int) and g == 0):
                        segment_edges(g - 1, (r - 1) % R)
                    pe.wait_ge(s_["h2_ok"], g + 1)
                    for k in range(G // 2):
                        ins = pe.matmul(ps[4][:, 2 * k:2 * k + 2], h2r[:, k * P:(k + 1) * P], W3t[:], start=True, stop=True)
                    ins.then_inc(s_["e_ps"], 1)

            attr_turn(0, 0, 0)
            attr_turn(1, 0, 1)
            first_layer(0, 0)
            turns(pe, NG // R, edges)
            segment_edges(NG - 1, R - 1)

        @block.vector
        def _(dve):
            steps = [0]

            def chain(ins):
                steps[0] += 1
                ins.then_inc(s_["dve"], 1)
                dve.wait_ge(s_["dve"], steps[0])

            def wide(a):
                return a[:].rearrange("p (b u) -> p b u", u=1).to_broadcast([P, NB, D])

            dve.memset(X[:], 0.0)
            dve.memset(dstI, PAD_DST)
            dve.memset(srcI, 0)
            dve.memset(wI, 0)
            chain(dve.memset(tyI, 0))
            dve.sem_inc(s_["zero_ok"], 1)
            dve.memset(pre[:], 0.0)
            dve.memset(W2n[:], 0.0)
            dve.memset(W3n[:], 0.0)
            chain(dve.memset(Web[:], 0.0))
            dve.sem_inc(s_["zero_ok"], 1)
            dve.wait_ge(s_["pool_const"], 7)
            dve.tensor_copy(iotaN[:], iotaI[:])
            chain(dve.tensor_copy(iotaP[:], iotaPi[:]))
            dve.tensor_scalar(junkP[:], iotaP[:], float(NP), None, ALU.add)
            chain(dve.tensor_copy(stepN[:], tile_i[:]))
            dve.sem_inc(s_["const_ok"], 1)
            dve.wait_ge(s_["w_in"], 16 * 5)
            for half, wv in enumerate((srcT, rowT)):
                v = wv[0:DA, 0:D * NBASE].bitcast(F32).rearrange("i (o b) -> i o b", b=NBASE)
                c3 = linB[:].rearrange("i (u b) -> i u b", u=1).to_broadcast([DA, D, NBASE])
                chain(dve.tensor_tensor(v, v, c3, ALU.mult))
                chain(dve.tensor_reduce(W0[:, half * D:(half + 1) * D], v, AX.X, ALU.add))
            dve.sem_inc(s_["w0_ok"], 1)
            dve.wait_ge(s_["edges_in"], 16 * 8)
            hi = TMP[:, 0:STEPS].bitcast(I32)
            dve.tensor_scalar(hi, srcI, 7, None, ALU.logical_shift_right)
            chain(dve.tensor_scalar(srcI, srcI, P - 1, None, ALU.bitwise_and))
            chain(dve.scalar_tensor_tensor(srcI, srcI, float(NB), hi, ALU.mult, ALU.add))
            dve.sem_inc(s_["src_rows"], 1)
            dv = dstI.rearrange("p (c j) -> p c j", j=P)
            dve.tensor_scalar(edgeB[:, 0, :], dv[:, :, 0], 7, None, ALU.logical_shift_right)
            chain(dve.tensor_scalar(edgeB[:, 1, :], dv[:, :, P - 1], 7, None, ALU.logical_shift_right))
            chain(dve.tensor_copy(blo[:], edgeB[:, 0, :]))
            chain(dve.tensor_copy(cnt[:], edgeB[:, 1, :]))
            chain(dve.scalar_tensor_tensor(cnt[:], cnt[:], 1.0, blo[:], ALU.add, ALU.subtract))
            chain(dve.tensor_reduce(tot[:], cnt[:], AX.X, ALU.add))
            dve.sem_inc(s_["base_mm"], 1)
            dve.wait_ge(s_["base_mm"], 2)
            chain(dve.tensor_copy(start[:, 0:1], ps[4][:, 0:1]))
            for c in range(1, NC):
                chain(dve.tensor_tensor(start[:, c:c + 1], start[:, c - 1:c], cnt[:, c - 1:c], ALU.add))
            chain(dve.tensor_tensor(q[:], blo[:], start[:], ALU.subtract))
            dve.sem_inc(s_["tiles_ok"], 1)
            dve.wait_ge(s_["start_in"], 16)
            for c in range(NC):
                chain(dve.tensor_scalar(leq, startB, stepN[:, c:c + 1], None, ALU.is_le))
                chain(dve.tensor_reduce(cnt[:, c:c + 1], leq, AX.X, ALU.add))
            chain(dve.tensor_scalar(tile_i[:], cnt[:], -1.0, None, ALU.add))

            def columns(c):
                dve.tensor_copy(stepc[:], stepN[:, bass.ds(c, 1)])
                dve.tensor_copy(tcol[:], tile_i[:, bass.ds(c, 1)]).then_inc(s_["tcol_ok"], 1)
                dve.wait_ge(s_["tcol_ok"], c + 1)
                dve.wait_ge(s_["stair_g"], c * 48 + 48)
                wait(dve, s_["stair_out"], c * 64)
                dve.tensor_tensor(blkf[:], qg[:], stepc[:], ALU.add)
                dve.tensor_copy(fld[:, 0:P], rg[:, 0:P])
                dve.tensor_copy(fld16[:, 0, :], rg[:, 0:P])
                dve.tensor_copy(fld[:, P:2 * P], rg[:, P:2 * P])
                dve.tensor_copy(fld[:, 3 * P:4 * P], rg[:, 3 * P:4 * P]).then_inc(s_["stair_d"], 1)
                dve.wait_ge(s_["stair_d"], c * 3 + 1)
                dve.tensor_scalar(blki[:], blkf[:], float(D), None, ALU.mult)
                dve.tensor_scalar(nblk[:], blkf[:], -float(P), None, ALU.mult)
                dve.scalar_tensor_tensor(fld[:, 3 * P:4 * P], fld[:, 0:P], float(NREL), fld[:, 3 * P:4 * P],
                                         ALU.mult, ALU.add).then_inc(s_["stair_d"], 1)
                dve.wait_ge(s_["stair_d"], c * 3 + 2)
                dve.tensor_scalar(fld16[:, 1, :], fld[:, P:2 * P], nblk[:, 0:1], None, ALU.add)
                dve.tensor_scalar(fld[:, P:2 * P], fld[:, P:2 * P], nblk[:, 0:1], None, ALU.add).then_inc(s_["stair_f"], 1)
                dve.wait_ge(s_["stair_T"], c + 1)
                dve.tensor_copy(srcT[:, bass.ds(c * P, P)], ps[4][:, 0:P])
                dve.tensor_copy(relT[:, bass.ds(c * P, P)], ps[4][:, P:2 * P])
                dve.tensor_copy(wT[:, bass.ds(c * P, P)], ps[4][:, 2 * P:3 * P])
                dve.tensor_copy(rowT[:, bass.ds(c * P, P)], ps[4][:, 3 * P:4 * P]).then_inc(s_["stair_d"], 1)
                dve.wait_ge(s_["stair_d"], c * 3 + 3)

            turns(dve, NC, columns)
            dve.sem_inc(s_["stair_done"], 1)
            dve.wait_ge(s_["x_in"], 32)
            chain(dve.memset(H[:], 1.0))

            def layernorm(n):
                chain(dve.tensor_reduce(s1[:], Xv, AX.X, ALU.add))
                chain(dve.tensor_scalar(s1[:], s1[:], 1.0 / D, None, ALU.mult))
                chain(dve.tensor_tensor(Hv, Xv, wide(s1), ALU.subtract))
                chain(dve.tensor_tensor(TMPv, Hv, Hv, ALU.mult))
                chain(dve.tensor_reduce(s2[:], TMPv, AX.X, ALU.add))
                chain(dve.tensor_scalar(s2[:], s2[:], 1.0 / D, LN_EPS, ALU.mult, ALU.add))
                dve.sem_inc(s_["ln_var"], 1)
                dve.wait_ge(s_["ln_std"], n)
                chain(dve.reciprocal(s1[:], s3[:]))
                chain(dve.tensor_tensor(Hv, Hv, wide(s1), ALU.mult))
                chain(dve.tensor_scalar(Hv, Hv, 0.0, None, ALU.max))
                dve.sem_inc(s_["ln_ok"], 1)

            def projected(n, move):
                def group(j):
                    for b in range(BG):
                        if b % 2 == 0:
                            wait(dve, tab_out[b // 2], (n * NJ + j) * 16)
                        dve.wait_ge(s_["proj_ps"], (n * NJ + j) * BG + b + 1)
                        move(j, b, 2 + 2 * (b % 2)).then_inc(s_["proj_mv"], 1)

                turns(dve, NJ, group)

            def move0(j, b, bank):
                dve.tensor_copy(TO[:, b * D:(b + 1) * D], ps[bank][:, 0:D])
                return dve.tensor_copy(AG[:, bass.ds(j * (BG * D) + b * D, D)], ps[bank][:, D:2 * D])

            def move1(j, b, bank):
                w = NREL * D
                return dve.tensor_copy(TO[:, b * w:b * w + 512], ps[bank][:])

            def move3(j, b, bank):
                dve.tensor_copy(TO[:, b * 2 * D:(b + 1) * 2 * D], ps[bank][:, 0:2 * D])
                xb = X[:, bass.ds(j * (BG * D) + b * D, D)]
                dve.tensor_tensor(xb, xb, ps[bank][:, 2 * D:3 * D], ALU.add)
                return dve.tensor_copy(AG[:, bass.ds(j * (BG * D) + b * D, D)], ps[bank][:, 3 * D:4 * D])

            def steps_of(t, g, width=P):
                return t[:, bass.ds(g * G, G)].rearrange("p (k u) -> p k u", u=1).to_broadcast([P, G, width])

            def steps_of1(t):
                return t[:].rearrange("p (k u) -> p k u", u=1).to_broadcast([P, G, D])

            nview = iotaN[:].rearrange("p (u n) -> p u n", u=1).to_broadcast([P, G, P])

            def one_hot(n, g, h):
                wait(dve, s_["mm_ok"], n * NG + g + (R - 1))
                dve.tensor_tensor(S[:, h, :, :], steps_of(relT, g), nview, ALU.is_equal).then_inc(s_["S_ok"], 1)

            regs = [dve.alloc_register(f"dve_blk{k}") for k in range(G)]

            def accumulate(n, i, r, acc):
                dve.reg_load(regs, blkR[0:1, bass.ds(i * (R * G) + r * G, G)])
                cols = [dve.snap(x_, min_val=0, max_val=(NODE_BLOCKS - 1) * D) for x_ in regs]
                dve.wait_ge(s_["mm_ok"], i * R + (n * NG + r + R + 1))
                for k in range(G):
                    if isinstance(i, int) and n == 0 and (i * R + r) * G + k < 2:
                        pass
                    else:
                        dve.wait_ge(s_["acc_ok"], i * (R * G) + ((n * NG + r) * G + k - 1))
                    a = (acc, TMP)[k % 2][:, bass.ds(cols[k], D)]
                    dve.tensor_tensor(a, a, ps[6 + r % 2][:, k * D:(k + 1) * D], ALU.add).then_inc(s_["acc_ok"], 1)

            def finish(n, acc):
                dve.wait_ge(s_["acc_ok"], (n + 1) * NG * G)
                chain(dve.tensor_tensor(acc[:], acc[:], TMP[:], ALU.add))

            def message_pass(n, acc):
                chain(dve.memset(TMP[:], 0.0))
                one_hot(n, 0, 0)

                def groups(i):
                    for r in range(R):
                        g = i * R + r
                        if not (isinstance(g, int) and g == NG - 1):
                            one_hot(n, g + 1, (r + 1) % 2)
                        accumulate(n, i, r, acc)

                turns(dve, NG // R, groups)
                finish(n, acc)

            layernorm(1)
            projected(0, move0)
            dve.wait_ge(s_["blk_in"], 16)
            message_pass(0, AG)
            chain(dve.tensor_tensor(TMPv, AGv, AGv, ALU.mult))
            chain(dve.tensor_reduce(s2[:], TMPv, AX.X, ALU.add))
            dve.sem_inc(s_["nrm_in"], 1)
            dve.wait_ge(s_["nrm_out"], 1)
            chain(dve.tensor_scalar(s1[:], s3[:], L2_EPS, None, ALU.max))
            chain(dve.reciprocal(s1[:], s1[:]))
            chain(dve.tensor_tensor(AGv, AGv, wide(s1), ALU.mult))
            chain(dve.tensor_tensor(Xv, Xv, AGv, ALU.add))
            layernorm(2)
            projected(1, move1)
            message_pass(1, X)
            layernorm(3)
            dve.wait_ge(s_["tabs_zero"], 16 * NH * NT)
            chain(dve.tensor_copy(AGv, Hv))
            mask = lower[:].rearrange("p (u n) -> p u n", u=1).to_broadcast([P, G, P])
            for m in range(NH):
                dve.sem_inc(s_["hop_go"], 1)

                def spreader(g, i, r):
                    dve.wait_ge(rows_in[r], (m * (NG // R) + i + 1) * 32)
                    dve.tensor_scalar(ST[:, r % 2, :, :].rearrange("p k e -> p (k e)"), raw[:, r, 0, :], iotaP[:, 0:1], None,
                                      ALU.is_equal).then_inc(s_["hop_ST"], 1)

                def same_src(g, r):
                    wait(dve, s_["sum_ps"], m * NG + g - 1)
                    dve.tensor_tensor(S[:, r % 2, :, :], raw[:, r, 1, :].rearrange("p (k e) -> p k e", k=G), steps_of(srcT, g),
                                      ALU.is_equal).then_inc(s_["hop_M"], 1)

                def targets(g, h):
                    dve.wait_ge(s_["hop_M"], g + 1)
                    wait(dve, s_["dup_ok"], g * 4)
                    later = TMP[:, 0:G * P].rearrange("p (k e) -> p k e", k=G)
                    dve.tensor_tensor(later, S[:, h, :, :], mask, ALU.mult).then_inc(s_["dup_ok"], 1)
                    dve.tensor_scalar(away[:], srcT[:, bass.ds(g * G, G)], -1.0, junkP[:, 0:1], ALU.mult, ALU.add)
                    dve.wait_ge(s_["dup_ok"], g * 4 + 1)
                    dve.tensor_reduce(dups[:], later, AX.X, ALU.add).then_inc(s_["dup_ok"], 1)
                    dve.wait_ge(s_["dup_ok"], g * 4 + 2)
                    dve.scalar_tensor_tensor(away[:], dups[:], 0.5, away[:], ALU.is_gt, ALU.mult).then_inc(s_["dup_ok"], 1)
                    dve.wait_ge(s_["dup_ok"], g * 4 + 3)
                    dve.tensor_tensor(rowT[:, bass.ds(g * G, G)], away[:], srcT[:, bass.ds(g * G, G)], ALU.add).then_inc(s_["dup_ok"], 1)

                def weighted(g, r):
                    dve.wait_ge(s_["msg_ps"], m * NG + g + 1)
                    dve.tensor_tensor(pre[:, r % 2, :].rearrange("p (k f) -> p k f", f=D),
                                      ps[r % 2][:].rearrange("p (k f) -> p k f", f=D),
                                      steps_of(wT, g, D), ALU.mult).then_inc(s_["msg_ok"], 1)

                def ahead(g, r):
                    same_src(g, r)
                    if m == 0:
                        targets(g, r % 2)
                    weighted(g, r)

                def groups(i):
                    for r in range(R):
                        g = i * R + r
                        if not (isinstance(g, int) and g == NG - 1):
                            ahead(g + 1, (r + 1) % R)
                        if not (isinstance(g, int) and g >= NG - 2):
                            spreader(g + 2, i if r < R - 2 else i + 1, (r + 2) % R)

                spreader(0, 0, 0)
                ahead(0, 0)
                spreader(1, 0, 1)
                turns(dve, NG // R, groups)
                dve.wait_ge(s_["sum_ps"], (m + 1) * NG)
                dve.sem_inc(s_["hop_go"], 1)
                for t in range(NT):
                    dve.wait_ge(sum_in[t % 2], (m * (NT // 2) + t // 2 + 1) * 16)
                    part = (TMP[:], TO[:, 0:NB * D])[t % 2]
                    if t == 0:
                        chain(dve.tensor_copy(AG[:], part))
                    else:
                        chain(dve.tensor_tensor(AG[:], AG[:], part, ALU.add))
                    dve.sem_inc(s_["sum_mv"], 1)
                chain(dve.tensor_tensor(Hv, Hv, AGv, ALU.add))
            chain(dve.scalar_tensor_tensor(Xv, Hv, 0.25, Xv, ALU.mult, ALU.add))
            layernorm(4)
            projected(2, move3)
            chain(dve.memset(TMP[:], 0.0))

            def spreader(g, i, r):
                dve.wait_ge(rows_in[r], NH * (NG // R) * 32 + (i + 1) * 16)
                dve.tensor_scalar(ST[:, r % 2, :, :].rearrange("p k e -> p (k e)"), raw[:, r, 0, :], iotaP[:, 0:1], None,
                                  ALU.is_equal).then_inc(s_["ST_ok"], 1)

            def rows_of(r, part):
                return gat[:, r, :].rearrange("p (k f) -> p k f", f=2 * D)[:, :, part * D:(part + 1) * D]

            def first_layer(g, i, r):
                dve.wait_ge(s_["pre_ps"], g + 1)
                dve.wait_ge(gather_ok[r], i * (16 * G) + (EDGE * (NG // R) + 1) * 16 * G)
                dve.tensor_tensor(pre[:, 0, :].rearrange("p (k f) -> p k f", f=D), ps[1][:].rearrange("p (k f) -> p k f", f=D),
                                  rows_of(r, 1), ALU.add).then_inc(s_["pre_ok"], 1)

            def edges(i):
                for r in range(R):
                    g = i * R + r
                    if not (isinstance(g, int) and g < 2):
                        accumulate(EDGE, i if r >= 2 else i - 1, (r + 2) % R, X)
                    dve.wait_ge(s_["h1_sb"], g + 1)
                    dve.scalar_tensor_tensor(h1r[:], h1[:], NEG_SLOPE, h1[:], ALU.mult, ALU.max).then_inc(s_["h1_ok"], 1)
                    one_hot(EDGE, g, r % 2)
                    if not (isinstance(g, int) and g >= NG - 2):
                        spreader(g + 2, i if r < R - 2 else i + 1, (r + 2) % R)
                    dve.wait_ge(s_["h2_sb"], g + 1)
                    dve.scalar_tensor_tensor(h2r[:], h2[:], NEG_SLOPE, h2[:], ALU.mult, ALU.max).then_inc(s_["h2_ok"], 1)
                    if not (isinstance(g, int) and g == NG - 1):
                        first_layer(g + 1, i if r < R - 1 else i + 1, (r + 1) % R)
                    dve.wait_ge(s_["e_ps"], g + 1)
                    dve.tensor_scalar(esc[:], ps[4][:, 0:G], b3c[:, 0:1], 0.0, ALU.add, ALU.max).then_inc(s_["esc_ok"], 1)
                    dve.wait_ge(s_["esc_ok"], g + 1)
                    dve.tensor_tensor(rows_of(r, 0), rows_of(r, 0), steps_of1(esc), ALU.mult).then_inc(s_["ge_ok"], 1)

            spreader(0, 0, 0)
            first_layer(0, 0, 0)
            spreader(1, 0, 1)
            turns(dve, NG // R, edges)
            for r in (R - 2, R - 1):
                accumulate(EDGE, NG // R - 1, r, X)
            finish(EDGE, X)
            dve.sem_inc(s_["pass_ok"], 1)


_INS = ['x', 'src', 'dst', 'edge_attr_8', 'edge_type_16', 'edge_weight', 'L0_gnn_basis_msg_wt', 'L0_gnn_basis_msg_bias',
        'L0_gnn_basis_self_wt', 'L0_gnn_basis_self_bias', 'L0_gnn_lin_comb', 'L1_gnn_weight', 'L3_gnn_W_src', 'L3_gnn_b_src',
        'L3_gnn_W_tgt', 'L3_gnn_b_tgt', 'L3_gnn_W_edge', 'L3_gnn_b_edge', 'L3_gnn_W1', 'L3_gnn_b1', 'L3_gnn_W2', 'L3_gnn_b2',
        'L3_gnn_W3', 'L3_gnn_b3']


def kernel(**inputs):
    import numpy as _np
    import concourse.bacc as _bacc
    from concourse import mybir as _mybir
    from concourse.bass_utils import run_bass_kernel_spmd as _run

    nc = _bacc.Bacc("TRN2", target_bir_lowering=False, num_devices=1)
    arrays, args = {}, []
    for name in _INS:
        a = _np.ascontiguousarray(inputs[name])
        arrays[f"in_{name}_dram"] = a
        args.append(nc.dram_tensor(f"in_{name}_dram", a.shape, _mybir.dt.from_np(a.dtype), kind="ExternalInput").ap())
    o = nc.dram_tensor("out_0_dram", inputs['x'].shape, _mybir.dt.float32, kind="ExternalOutput").ap()
    gnn_kernel(nc, *args, o)
    r = _run(nc, [arrays], core_ids=[0])
    return r.results[0]["out_0_dram"]
```

```python
from contextlib import ExitStack

import concourse.bass as bass
from concourse import mybir

F32 = mybir.dt.float32
I32 = mybir.dt.int32
I16 = mybir.dt.int16
ALU = mybir.AluOpType
ACT = mybir.ActivationFunctionType
AX = mybir.AxisListType

P = 128
LN_EPS = 1e-5
L2_EPS = 1e-12
NEG_SLOPE = 0.01
G = 8
R = 4


def gnn_kernel(nc, x, src, dst, edge_attr, etype, eweight, msg_wt, msg_b, self_wt, self_b, lin, rel_w,
               W_src, b_src, W_tgt, b_tgt, W_edge, b_edge, W1, b1, W2, b2, W3, b3, out):
    N, D = x.shape
    E = src.shape[0]
    EA = edge_attr.shape[1]
    NREL = rel_w.shape[0]
    NBASE = msg_wt.shape[2]
    H2 = W2.shape[0]
    NODE_BLOCKS = -(-N // P)
    BG = 4
    NJ = -(-NODE_BLOCKS // BG)
    NB = NJ * BG
    NP = NB * P
    TILES = -(-E // P)
    assert NJ % 2 == 1 and NJ >= 5
    NC = -(-(TILES + NODE_BLOCKS - 1) // P)
    STEPS = NC * P
    assert STEPS % (G * R) == 0 and D == 64 and G * EA == 64 and H2 == 32
    NG = STEPS // G
    PAD_DST = NODE_BLOCKS * P - 1
    assert PAD_DST >= N
    DA = D + 1
    NH = 3
    assert NC % 2 == 1 and NC >= 5
    assert NB * P + P < 2 ** 15
    LN_SPLIT = 3 * BG
    RW = (4 + EA) * P + 1
    NT = G
    ACC_ROWS = NP + P
    EDGE = 2

    with ExitStack() as ctx:
        def sb(name, shape, dt=F32):
            return ctx.enter_context(nc.sbuf_tensor(name, shape, dt))

        def sem(name):
            return ctx.enter_context(nc.semaphore(name))

        def dram(name, shape, dt=F32):
            return nc.dram_tensor(name, shape, dt).ap()

        rec_d = dram("rec_d", (STEPS, RW), I32)
        start_d = dram("start_d", (STEPS,))
        blk_d = dram("blk_d", (STEPS,), I32)
        rel_d = dram("rel_d", (STEPS, P), I16)
        attr_s = dram("attr_s", (NG, P, G * EA))
        tab0 = dram("tab0", (NP, D))
        tab1 = dram("tab1", (NP, NREL * D))
        acc_d = [[dram(f"acc_d{m}_{t}", (ACC_ROWS, D)) for t in range(NT)] for m in range(NH)]
        src_d = dram("src_d", (STEPS, P), I16)
        tab3 = dram("tab3", (NP, 2 * D))

        X = sb("X", [P, NB * D])
        H = sb("H", [P, NB * DA])
        pair = sb("pair", [P, 2, NB * D])
        TMP = pair[:, 0, :]
        AG = pair[:, 1, :]
        Xv = X[:].rearrange("p (b f) -> p b f", f=D)
        Hv = H[:].rearrange("p (b f) -> p b f", f=DA)[:, :, 0:D]
        TMPv = TMP[:].rearrange("p (b f) -> p b f", f=D)
        AGv = AG[:].rearrange("p (b f) -> p b f", f=D)
        s1 = sb("s1", [P, NB])
        s2 = sb("s2", [P, NB])
        s3 = sb("s3", [P, NB])
        srcT = sb("srcT", [P, STEPS], I32)
        rowT = sb("rowT", [P, STEPS], I32)
        relT = sb("relT", [P, STEPS])
        wT = sb("wT", [P, STEPS])
        blkR = sb("blkR", [1, STEPS], I32)
        idx = sb("idx", [P, R, G], I32)
        gat = sb("gat", [P, R, G * 2 * D])
        S = sb("S", [P, 2, G, P])
        ST = sb("ST", [P, 2, G, P])
        attrG = sb("attrG", [P, R, G * EA])
        attrT = sb("attrT", [G * EA, 2, P])
        pre = sb("pre", [P, 2, G * D])
        h1 = sb("h1", [P, G * D])
        h1r = sb("h1r", [P, G * D])
        h2 = sb("h2", [2 * H2, G * D])
        h2r = sb("h2r", [2 * H2, G * D])
        esc = sb("esc", [P, G])
        dups = sb("dups", [P, G])
        away = sb("away", [P, G])
        junkP = sb("junkP", [P, 1])
        TO = sb("TO", [P, BG * NREL * D])
        HS = sb("HS", [P, 2, BG * DA])
        HT = sb("HT", [DA, 2, BG * P])
        raw = TO[:, 0:R * 2 * G * P // 2].bitcast(I16).rearrange("p (r t e) -> p r t e", r=R, t=2)
        iotaN = sb("iotaN", [P, P])
        iotaI = sb("iotaI", [P, P], I32)
        iotaP = sb("iotaP", [P, 1])
        iotaPi = sb("iotaPi", [P, 1], I32)
        ident = sb("ident", [P, P])
        stepN = sb("stepN", [P, NC])
        lower = sb("lower", [P, P])
        linB = sb("linB", [DA, NBASE])
        W0 = sb("W0", [DA, 2 * D])
        WR = sb("WR", [D, NREL * D])
        As = sb("As", [D, DA])
        At = sb("At", [D, DA])
        Ae = sb("Ae", [D, EA])
        be = sb("be", [D, 1])
        W1n = sb("W1n", [D, 3 * D])
        W1t = sb("W1t", [D, 4 * D])
        W2n = sb("W2n", [2 * H2, P])
        W3n = sb("W3n", [2, 2 * H2])
        W2t = sb("W2t", [P, 2 * H2])
        W3t = sb("W3t", [2 * H2, 2])
        W4 = sb("W4", [DA, 4 * D])
        We = sb("We", [EA, D])
        Web = sb("Web", [G * EA, G, D])
        b1c = sb("b1c", [P, 1])
        b1s = sb("b1s", [P, 1])
        b2c = sb("b2c", [2 * H2, 1])
        b3c = sb("b3c", [P, 1])
        dstI = TO[:, BG * D:BG * D + STEPS].bitcast(I32)
        srcI = TO[:, BG * D + STEPS:BG * D + 2 * STEPS].bitcast(I32)
        wI = wT[:].bitcast(I32)
        tyI = relT[:].bitcast(I32)
        rec_buf = (gat[:, 0:2, :].rearrange("p r f -> p (r f)"), S[:].rearrange("p h k n -> p (h k n)"))
        startB = rec_buf[0][:, 0:STEPS]
        blo = sb("blo", [P, NC])
        cnt = sb("cnt", [P, NC])
        edgeB = sb("edgeB", [P, 2, NC], I32)
        start = sb("start", [P, NC])
        q = sb("q", [P, NC])
        tot = sb("tot", [P, 1])
        tile_i = sb("tile_i", [P, NC], I32)
        tcol = sb("tcol", [P, 2], I32)
        nblk = sb("nblk", [P, 1])
        blkf = sb("blkf", [P, 1])
        blki = sb("blki", [P, 1], I32)
        fld = gat[:, 2, 0:4 * P]
        fld16 = gat[:, 2, 4 * P:5 * P].bitcast(I16).rearrange("p (t e) -> p t e", t=2)
        eo = gat[:, 3, :]

        ps = [ctx.enter_context(nc.psum_tensor(f"ps{i}", [P, 512], F32)) for i in range(8)]

        SEMS = """
            src_rows gathers_begun turns_begun zero_ok pool_const const_ok edges_in w_in w0_ok rel_in mlp_in mlp_T
            mlp_Tc mlp_mm mlp_c web_in rec_out attr_out start_out start_in base_mm tcol_ok stair_f stair_T stair_e
            stair_out tiles_ok blk_in stair_done dve stair_d x_in ln_var ln_std ln_ok hs_ok hT_ps ht_ok proj_ps
            proj_mv nrm_in nrm_out tabs_zero hop_done hop_ST hop_M msg_ps msg_ok sum_ps rows_ok dup_ok sum_mv idx_ok
            mm_ok S_ok acc_ok esc_ok ST_ok aT_ps aT_ok pre_ps pre_ok h1_ps h1_sb h1_ok h2_ps h2_sb h2_ok e_ps ge_ok
            pass_ok out_in
            """.split()
        sems = {n: sem(n) for n in SEMS}
        gather_ok = [sem(f"gather_ok{r}") for r in range(R)]
        scat_ok = [sem(f"scat_ok{h}") for h in range(2)]
        rows_in = [sem(f"rows_in{r}") for r in range(R)]
        attr_in = [sem(f"attr_in{r}") for r in range(R)]
        tab_out = [sem(f"tab_out{h}") for h in range(2)]

        def has_nodes(j, b):
            return not isinstance(j, int) or j * BG + b < NODE_BLOCKS

        def blocks_done(j, b):
            return BG - b if not has_nodes(j, b + 1) else 1

        def sum_buf(t):
            return AG if t == 0 else (TMP, gat[:].rearrange("p r f -> p (r f)")[:, 0:NB * D])[t % 2]

        def sum_sem(t):
            return 0 if t == 0 else 1 + t % 2

        stair_g = [sem(f"stair_g{h}") for h in range(2)]
        sum_in = [[sem(f"sum_in{b}_{h}") for h in range(2)] for b in range(3)]

        block = ctx.enter_context(nc.Block())
        s_ = sems
        FULL = E // STEPS
        REST = E - FULL * STEPS
        NFULL = N // P
        PZ = next(u for u in range(1, 64) if ACC_ROWS % (P * u) == 0 and ACC_ROWS // (P * u) <= G)
        NREST = N - NFULL * P
        TF = E // P
        EREST = (E - TF * P) * EA
        assert 0 < EREST and STEPS - TF - 1 <= P and P * EA <= 2 * G * D

        def wait(eng, semaphore, value):
            if not isinstance(value, int) or value > 0:
                eng.wait_ge(semaphore, value)

        def turns(eng, n, body):
            body(0)
            with eng.Fori(1, n - 1) as i:
                body(i)
            body(n - 1)

        def column_turns(eng, body):
            body(0, 0)
            with eng.Fori(0, (NC - 3) // 2) as i:
                for h in range(2):
                    body(i * 2 + (h + 1), 1 - h)
            body(NC - 2, 1)
            body(NC - 1, 0)

        @block.sync
        def _(sp):
            sp.wait_ge(s_["zero_ok"], 1)
            for dstb, a in ((dstI, dst), (srcI, src), (wI, eweight.bitcast(I32)), (tyI, etype)):
                sp.dma_start(dstb[0:FULL, :], a[0:FULL * STEPS].rearrange("(p j) -> p j", j=STEPS)).then_inc(s_["edges_in"], 16)
                sp.dma_start(dstb[FULL:FULL + 1, 0:REST], a[FULL * STEPS:E].rearrange("(p j) -> p j", p=1)).then_inc(s_["edges_in"], 16)
            sp.dma_start(Xv[:, 0:NFULL, :], x[0:NFULL * P, :].rearrange("(b p) f -> p b f", p=P)).then_inc(s_["x_in"], 16)
            sp.dma_start(Xv[0:NREST, NFULL, :], x[NFULL * P:N, :]).then_inc(s_["x_in"], 16)
            for half, (wt, bias) in enumerate(((msg_wt, msg_b), (self_wt, self_b))):
                wv = srcT if half == 0 else rowT
                sp.dma_start(wv[0:D, 0:D * NBASE].bitcast(F32), wt.rearrange("i o b -> i (o b)")).then_inc(s_["w_in"], 16)
                sp.dma_start(wv[D:DA, 0:D * NBASE].bitcast(F32), bias.rearrange("(u o) b -> u (o b)", u=1)).then_inc(s_["w_in"], 16)
            sp.dma_start(linB[:], lin.to_broadcast([DA, NBASE])).then_inc(s_["w_in"], 16)
            sp.dma_start(WR[:].rearrange("i (r o) -> i r o", r=NREL), rel_w.rearrange("r i o -> i r o")).then_inc(s_["rel_in"], 16)
            col = lambda a: a.rearrange("(p u) -> p u", u=1)
            sp.wait_ge(s_["zero_ok"], 2)
            for o, i in ((As[:, 0:D], W_src), (As[:, D:DA], col(b_src)), (At[:, 0:D], W_tgt), (At[:, D:DA], col(b_tgt)),
                         (Ae[:], W_edge), (be[:], col(b_edge)), (W1n[:], W1),
                         (W2n[0:H2, 0:D], W2), (W2n[H2:2 * H2, D:P], W2),
                         (W3n[0:1, 0:H2], W3), (W3n[1:2, H2:2 * H2], W3),
                         (b1s[0:D, :], col(b1)), (b1s[D:P, :], col(b1)), (b2c[0:H2, :], col(b2)), (b2c[H2:2 * H2, :], col(b2)),
                         (b3c[:], b3.rearrange("(u v) -> u v", u=1).to_broadcast([P, 1]))):
                sp.dma_start(o, i).then_inc(s_["mlp_in"], 16)
            attrs = rec_d[:, 4 * P:(4 + EA) * P]
            flat = edge_attr.bitcast(I32).rearrange("e a -> (e a)")
            for t0, t1 in ((0, TF // 2), (TF // 2, TF)):
                sp.dma_start(attrs[t0:t1, :], flat[t0 * P * EA:t1 * P * EA].rearrange("(t j) -> t j", j=P * EA)).then_inc(s_["rec_out"], 16)
                if t0 == 0:
                    sp.wait_ge(s_["tiles_ok"], 1)
                    sp.dma_start(start_d.rearrange("(p c) -> p c", c=NC), start[:]).then_inc(s_["start_out"], 16)
                    sp.wait_ge(s_["start_out"], 16)
                    sp.dma_start(startB, start_d.rearrange("(u s) -> u s", u=1).to_broadcast([P, STEPS])).then_inc(s_["start_in"], 16)
            sp.dma_start(attrs[TF:TF + 1, 0:EREST], flat[TF * P * EA:E * EA].rearrange("(u j) -> u j", u=1)).then_inc(s_["rec_out"], 16)
            zeros = pre[:].rearrange("p h f -> p (h f)").bitcast(I32)
            sp.dma_start(attrs[TF:TF + 1, EREST:P * EA], zeros[0:1, 0:P * EA - EREST]).then_inc(s_["rec_out"], 16)
            sp.dma_start(attrs[TF + 1:STEPS, :], zeros[0:STEPS - TF - 1, 0:P * EA]).then_inc(s_["rec_out"], 16)
            sp.dma_start(rec_d.rearrange("(p c) j -> p c j", c=NC)[:, :, RW - 1:RW], q[:].bitcast(I32).rearrange("p (c u) -> p c u", u=1),
                         allow_slow_non_contiguous=True).then_inc(s_["rec_out"], 16)
            sp.wait_ge(s_["src_rows"], 1)
            for f, b in enumerate((srcI, dstI, wI, tyI)):
                sp.dma_start(rec_d.rearrange("(p c) j -> p c j", c=NC)[:, :, f * P:(f + 1) * P],
                             b.rearrange("p (c j) -> p c j", j=P)).then_inc(s_["rec_out"], 16)

            def tables(n, tab, width):
                hb = BG // 2

                def group(j):
                    for h in range(2):
                        sp.wait_ge(s_["proj_mv"], (n * NJ + j) * BG + (h + 1) * hb)
                        if not isinstance(j, int):
                            sp.sem_inc(s_["turns_begun"], 1)
                        sp.dma_start(tab.rearrange("(p b) f -> p b f", p=P)[:, bass.ds(j * BG + h * hb, hb), :],
                                     TO[:, h * hb * width:(h + 1) * hb * width].rearrange("p (b f) -> p b f", f=width)).then_inc(tab_out[h], 16)

                turns(sp, NJ, group)

            tables(0, tab0, D)
            with sp.Fori(0, NC) as c:
                sp.wait_ge(s_["stair_f"], c + 1)
                sp.dma_start(rel_d[bass.ds(c * P, P), :], fld16[:, 1, :]).then_inc(s_["stair_out"], 16)
                sp.dma_start(src_d[bass.ds(c * P, P), :], fld16[:, 0, :]).then_inc(s_["stair_out"], 16)
                sp.dma_start(blk_d[bass.ds(c * P, P)].rearrange("(p u) -> p u", u=1), blki[:]).then_inc(s_["stair_out"], 16)
                sp.wait_ge(s_["stair_e"], c + 1)
                sp.dma_start(attr_s[bass.ds(c * (P // G), P // G), :, :].rearrange("g p m -> p g m"),
                             eo.rearrange("p (g m) -> p g m", m=G * EA)).then_inc(s_["attr_out"], 16)
            sp.wait_ge(s_["stair_out"], 48 * NC)
            sp.wait_ge(s_["attr_out"], 16 * NC)
            sp.dma_start(blkR[:], blk_d.rearrange("(u s) -> u s", u=1)).then_inc(s_["blk_in"], 16)
            for k in range(G):
                if k == 0:
                    sp.wait_ge(s_["mlp_c"], 3)
                sp.dma_start(Web[k * EA:(k + 1) * EA, k, :], We[:]).then_inc(s_["web_in"], 16)
            sp.wait_ge(s_["zero_ok"], 2)
            for m in range(NH):
                for t in range(NT):
                    sp.wait_ge(s_["mm_ok"], R + 1 + (m * NT + t) * ((NG - 2 * R) // (NH * NT)))
                    sp.dma_start(acc_d[m][t].rearrange("(p u b) f -> p u (b f)", p=P, u=PZ),
                                 pre[:, 0, 0:ACC_ROWS * D // (P * PZ)].rearrange("p (v w) -> p v w", v=1).to_broadcast([P, PZ, ACC_ROWS * D // (P * PZ)])).then_inc(s_["tabs_zero"], 16)
            tables(1, tab1, NREL * D)
            for h in range(2):
                sp.wait_ge(tab_out[h], 32 * NJ)
            for m in range(NH):
                def rows(i):
                    for r in range(R):
                        g = i * R + r
                        wait(sp, s_["hop_M"], m * NG + g - R + 1)
                        for t, tab in enumerate((rel_d, src_d)):
                            sp.dma_start(raw[:, r, t, :], tab[bass.ds(g * G, G), :].rearrange("(u k) e -> u (k e)", u=1)
                                         .to_broadcast([P, G * P])).then_inc(rows_in[r], 16)

                turns(sp, NG // R, rows)
                for h in range(2):
                    sp.wait_ge(scat_ok[h], (m + 1) * NG * 16 * (G // 2))
                sp.wait_ge(s_["hop_done"], m + 1)
                for t in range(NT):
                    for half in range(2):
                        if t >= 3:
                            sp.wait_ge(s_["sum_mv"], m * 2 * (NT - 1) + 2 * (t - 3) + half + 1)
                        blk0, blk1 = half * NB // 2, (half + 1) * NB // 2
                        sp.dma_start(sum_buf(t)[:, blk0 * D:blk1 * D].rearrange("p (b f) -> p b f", f=D),
                                     acc_d[m][t][0:NP, :].rearrange("(p b) f -> p b f", p=P)[:, blk0:blk1, :]).then_inc(sum_in[sum_sem(t)][half], 16)
            tables(2, tab3, 2 * D)
            sp.wait_ge(s_["proj_mv"], 3 * NJ * BG)

            def edge_rows(i):
                for r in range(R):
                    g = i * R + r
                    wait(sp, s_["ST_ok"], g - R + 1)
                    sp.dma_start(raw[:, r, 0, :], rel_d[bass.ds(g * G, G), :].rearrange("(u k) e -> u (k e)", u=1)
                                 .to_broadcast([P, G * P])).then_inc(rows_in[r], 16)
                    wait(sp, s_["aT_ps"], g - R + 1)
                    sp.dma_start(attrG[:, r, :], attr_s[bass.ds(g, 1), :, :].rearrange("g p m -> (g p) m")).then_inc(attr_in[r], 16)

            for h in range(2):
                sp.wait_ge(tab_out[h], 48 * NJ)
            turns(sp, NG // R, edge_rows)
            sp.wait_ge(s_["pass_ok"], 1)
            sp.dma_start(out[0:NFULL * P, :].rearrange("(b p) f -> p b f", p=P), Xv[:, 0:NFULL, :]).then_inc(s_["out_in"], 16)
            sp.dma_start(out[NFULL * P:N, :], Xv[0:NREST, NFULL, :]).then_inc(s_["out_in"], 16)
            sp.wait_ge(s_["out_in"], 32)

        @block.gpsimd
        def _(pool):
            pool.iota(iotaI[:], [[1, P]], base=0, channel_multiplier=0).then_inc(s_["pool_const"], 1)
            pool.iota(iotaPi[:], [[0, 1]], base=0, channel_multiplier=1).then_inc(s_["pool_const"], 1)
            pool.memset(ident[:], 0.0).then_inc(s_["pool_const"], 1)
            pool.memset(lower[:], 1.0).then_inc(s_["pool_const"], 1)
            pool.wait_ge(s_["pool_const"], 4)
            pool.affine_select(out=ident[:], in_=ident[:], compare_op=ALU.not_equal, fill=1.0, base=0,
                               pattern=[[-1, P]], channel_multiplier=1).then_inc(s_["pool_const"], 1)
            pool.affine_select(out=lower[:], in_=lower[:], compare_op=ALU.is_gt, fill=0.0, base=0,
                               pattern=[[1, P]], channel_multiplier=-1).then_inc(s_["pool_const"], 1)
            pool.iota(tile_i[:], [[P, NC]], base=0, channel_multiplier=1).then_inc(s_["pool_const"], 1)
            pool.wait_ge(s_["rec_out"], 16 * 10)

            def records(c, h):
                pool.wait_ge(s_["tcol_ok"], c + 1)
                if not isinstance(c, int):
                    pool.sem_inc(s_["gathers_begun"], 1)
                pool.indirect_dma_start(rec_buf[h][:, 0:RW].bitcast(I32), None, rec_d,
                                        bass.IndirectOffsetOnAxis(ap=tcol[:, h:h + 1], axis=0)).then_inc(stair_g[h], 16)

            column_turns(pool, records)

            def gathers(n, table, width):
                with pool.Fori(0, NG // R) as i:
                    for r in range(R):
                        pool.wait_ge(s_["idx_ok"], i * R + n * NG + r + 1)
                        pool.sem_inc(s_["gathers_begun"], 1)
                        for k in range(G):
                            pool.indirect_dma_start(gat[:, r, k * width:(k + 1) * width], None, table,
                                                    bass.IndirectOffsetOnAxis(ap=idx[:, r, k:k + 1], axis=0)).then_inc(gather_ok[r], 16)

            for h in range(2):
                pool.wait_ge(tab_out[h], 16 * NJ)
            pool.wait_ge(s_["attr_out"], 16 * NC)
            gathers(0, tab0, D)
            for h in range(2):
                pool.wait_ge(tab_out[h], 32 * NJ)
            gathers(1, tab1.rearrange("n (r f) -> (n r) f", f=D), D)
            pool.wait_ge(s_["tabs_zero"], 16 * NH * NT)
            for m in range(NH):
                def scatters(i):
                    for r in range(R):
                        g = i * R + r
                        pool.wait_ge(s_["rows_ok"], m * NG + g + 1)
                        if not isinstance(g, int):
                            pool.sem_inc(s_["gathers_begun"], 1)
                        for k in range(G):
                            if k % (G // 2) == 0:
                                h = k // (G // 2)
                                wait(pool, scat_ok[h], (m * NG + g) * 16 * (G // 2))
                                if not isinstance(g, int):
                                    pool.sem_inc(s_["gathers_begun"], 1)
                            pool.indirect_dma_start(acc_d[m][k], bass.IndirectOffsetOnAxis(ap=idx[:, r, k:k + 1], axis=0),
                                                    gat[:, r, k * D:(k + 1) * D], None, compute_op=ALU.add).then_inc(scat_ok[k // (G // 2)], 16)

                turns(pool, NG // R, scatters)
            for h in range(2):
                pool.wait_ge(tab_out[h], 48 * NJ)
            gathers(EDGE, tab3, 2 * D)

        @block.scalar
        def _(act):
            parts = [0]

            def std(blk0, blk1):
                parts[0] += 1
                act.wait_ge(s_["ln_var"], parts[0])
                act.activation(s3[:, blk0:blk1], s2[:, blk0:blk1], ACT.Sqrt).then_inc(s_["ln_std"], 1)

            def lengths(part, blk0, blk1):
                act.wait_ge(s_["nrm_in"], part)
                act.activation(s3[:, blk0:blk1], s2[:, blk0:blk1], ACT.Sqrt).then_inc(s_["nrm_out"], 1)

            std(0, LN_SPLIT)
            act.wait_ge(s_["mlp_T"], 1)
            act.copy(W1t[:], ps[0][0:D, 0:4 * D]).then_inc(s_["mlp_Tc"], 1)
            act.copy(W2t[:], ps[1][:, 0:2 * H2])
            act.copy(W3t[:], ps[1][0:2 * H2, P:P + 2]).then_inc(s_["mlp_Tc"], 2)
            act.wait_ge(s_["mlp_mm"], 1)
            act.wait_ge(s_["zero_ok"], 2)
            act.copy(W4[:], ps[2][0:DA, 0:4 * D]).then_inc(s_["mlp_c"], 1)
            act.activation(b1c[:], ps[3][:, 0:1], ACT.Identity, bias=b1s[:, 0:1]).then_inc(s_["mlp_c"], 1)
            act.copy(We[:], ps[3][0:EA, D:2 * D]).then_inc(s_["mlp_c"], 1)
            def turn(n, ln_parts):
                def stage(j, q):
                    wait(act, s_["hT_ps"], n * NJ + j - 1)
                    act.copy(HS[:, q, :], H[:, bass.ds(j * (BG * DA), BG * DA)]).then_inc(s_["hs_ok"], 1)

                def stationary(j, q):
                    act.wait_ge(s_["hT_ps"], n * NJ + j + 1)
                    wait(act, s_["proj_ps"], (n * NJ + j - 1) * BG)
                    act.copy(HT[:, q, :], ps[q][0:DA, :]).then_inc(s_["ht_ok"], 1)

                def move_pair(j, u):
                    if n != 1 or has_nodes(j, 2 * u):
                        wait(act, tab_out[u], (n * NJ + j) * 16)
                    if n == 1:
                        for b in (2 * u, 2 * u + 1):
                            if not has_nodes(j, b):
                                continue
                            act.wait_ge(s_["proj_ps"], (n * NJ + j) * BG + b + 1)
                            for w in range(2):
                                ins = act.copy(TO[:, b * NREL * D + w * 512:b * NREL * D + (w + 1) * 512], ps[2 + 2 * (b % 2) + w][:])
                            ins.then_inc(s_["proj_mv"], blocks_done(j, b))
                        return
                    act.wait_ge(s_["proj_ps"], (n * NJ + j) * BG + 2 * u + 2)
                    two = ps[2 + u][:, 0:2 * width].rearrange("p (b f) -> p b f", b=2)
                    cols = bass.ds(j * (BG * D) + 2 * u * D, 2 * D)
                    tw = width // 2
                    act.copy(TO[:, 2 * u * tw:2 * (u + 1) * tw].rearrange("p (b f) -> p b f", b=2), two[:, :, 0:tw])
                    if n == 0:
                        ins = act.copy(AG[:, cols].rearrange("p (b f) -> p b f", b=2), two[:, :, tw:2 * tw])
                    else:
                        for t in range(2):
                            ins = act.copy(pair[:, t, cols].rearrange("p (b f) -> p b f", b=2), two[:, :, tw + t * D:tw + (t + 1) * D])
                    ins.then_inc(s_["proj_mv"], 2)

                def move(j):
                    move_pair(j, 0)
                    move_pair(j, 1)

                width = (2 * D, NREL * D, 4 * D)[n]
                act.wait_ge(s_["ln_ok"], ln_parts - 1)
                stage(0, 0)
                stage(1, 1)
                stationary(0, 0)
                stationary(1, 1)
                stage(2, 0)
                move_pair(0, 0)
                if n == 1:
                    lengths(2, LN_SPLIT, NB)
                elif n == 2:
                    std(LN_SPLIT, NB)
                move_pair(0, 1)
                stationary(2, 0)
                if n == 1:
                    move_pair(1, 0)
                    std(LN_SPLIT, NB)
                act.wait_ge(s_["ln_ok"], ln_parts)
                stage(3, 1)
                if n != 1:
                    move_pair(1, 0)
                move_pair(1, 1)
                stationary(3, 1)
                stage(4, 0)
                move(2)
                with act.Fori(1, (NJ - 3) // 2) as i:
                    for h in range(2):
                        stationary(i * 2 + (h + 2), h)
                        stage(i * 2 + (h + 3), 1 - h)
                        move(i * 2 + (h + 1))
                stationary(NJ - 1, 0)
                move(NJ - 2)
                move(NJ - 1)

            std(LN_SPLIT, NB)
            turn(0, 2)
            def attributes(c):
                act.wait_ge(s_["stair_T"], c + 1)
                wait(act, s_["attr_out"], c * 16)
                for hb in range(2):
                    o = eo.rearrange("p (s a) -> p a s", a=EA)[:, 4 * hb:4 * hb + 4, :]
                    ins = act.copy(o, ps[5 + hb][:].rearrange("p (a s) -> p a s", a=4))
                ins.then_inc(s_["stair_e"], 1)

            turns(act, NC, attributes)

            def indices(n, table):
                with act.Fori(0, NG // R) as i:
                    for r in range(R):
                        act.wait_ge(s_["mm_ok"], i * R + n * NG + r + 1)
                        act.copy(idx[:, r, :], table[:, bass.ds(i * (R * G) + r * G, G)]).then_inc(s_["idx_ok"], 1)

            act.wait_ge(s_["stair_done"], 1)
            indices(0, srcT)
            lengths(1, 0, LN_SPLIT)
            std(0, LN_SPLIT)
            turn(1, 4)
            indices(1, rowT)
            std(0, NB)
            for m in range(NH):
                def out_rows(i):
                    for r in range(R):
                        g = i * R + r
                        act.wait_ge(s_["sum_ps"], m * NG + g + 1)
                        for h in range(2):
                            wait(act, scat_ok[h], (m * NG + g - R + 1) * 16 * (G // 2))
                        act.copy(idx[:, r, :], rowT[:, bass.ds(g * G, G)])
                        act.copy(gat[:, r, 0:G * D], ps[2 + r % 2][:]).then_inc(s_["rows_ok"], 1)

                turns(act, NG // R, out_rows)
            std(0, LN_SPLIT)
            turn(2, 7)
            for r in range(R):
                act.wait_ge(s_["mm_ok"], EDGE * NG + r + 1)
                act.copy(idx[:, r, :], srcT[:, r * G:(r + 1) * G]).then_inc(s_["idx_ok"], 1)

            def attr_turn(g, h):
                act.wait_ge(s_["aT_ps"], g + 1)
                act.copy(attrT[:, h, :], ps[5 * h][0:G * EA, 0:P]).then_inc(s_["aT_ok"], 1)

            def edges(i):
                for r in range(R):
                    g = i * R + r
                    if not (isinstance(g, int) and g >= NG - 2):
                        attr_turn(g + 2, r % 2)
                    act.wait_ge(s_["h1_ps"], g + 1)
                    act.activation(h1[:], ps[2][:], ACT.Identity, bias=b1c[:, 0:1]).then_inc(s_["h1_sb"], 1)
                    act.wait_ge(s_["h2_ps"], g + 1)
                    act.activation(h2[:], ps[3][0:2 * H2, :], ACT.Identity, bias=b2c[:, 0:1]).then_inc(s_["h2_sb"], 1)
                    q = (r - 1) % R
                    if isinstance(g, int) and (g == 0 or g - 1 + R >= NG):
                        continue
                    act.wait_ge(s_["mm_ok"], g + (EDGE * NG + R))
                    act.copy(idx[:, q, :], srcT[:, bass.ds((g + (R - 1)) * G, G)]).then_inc(s_["idx_ok"], 1)

            attr_turn(0, 0)
            attr_turn(1, 1)
            turns(act, NG // R, edges)

        @block.tensor
        def _(pe):
            pe.wait_ge(s_["const_ok"], 1)
            pe.sem_inc(s_["mm_ok"], R)
            pe.wait_ge(s_["base_mm"], 1)
            pe.matmul(ps[7][:, 0:1], lower[:], tot[:], start=True, stop=True).then_inc(s_["base_mm"], 1)
            pe.wait_ge(s_["mlp_in"], 16 * 16)
            for k in range(4):
                pe.transpose(ps[0][0:D, k * D:(k + 1) * D], W1n[:, min(k, 2) * D:min(k, 2) * D + D], ident[0:D, 0:D])
            pe.transpose(ps[1][:, 0:2 * H2], W2n[:], ident[0:2 * H2, 0:2 * H2])
            pe.transpose(ps[1][0:2 * H2, P:P + 2], W3n[:], ident[0:2, 0:2])
            pe.transpose(ps[2][0:DA, 0:D], As[:], ident[0:D, 0:D])
            pe.transpose(ps[2][0:DA, 2 * D:3 * D], At[:], ident[0:D, 0:D]).then_inc(s_["mlp_T"], 1)
            pe.wait_ge(s_["mlp_Tc"], 3)
            pe.matmul(ps[2][0:DA, D:2 * D], As[:], W1t[:, 0:D], start=True, stop=True)
            pe.matmul(ps[2][0:DA, 3 * D:4 * D], At[:], W1t[:, D:2 * D], start=True, stop=True)
            pe.matmul(ps[3][:, 0:1], W1t[:, 2 * D:4 * D], be[:], start=True, stop=True)
            pe.matmul(ps[3][0:EA, D:2 * D], Ae[:], W1t[:, 2 * D:3 * D], start=True, stop=True).then_inc(s_["mlp_mm"], 1)
            def project(n, w, width, k):
                def turn(j, q):
                    pe.wait_ge(s_["hs_ok"], n * NJ + j + 1)
                    wait(pe, s_["ht_ok"], n * NJ + j - 1)
                    for b in range(BG):
                        ins = pe.transpose(ps[q][0:DA, b * P:(b + 1) * P], HS[:, q, b * DA:(b + 1) * DA], ident[:])
                    ins.then_inc(s_["hT_ps"], 1)

                def products(j, q):
                    pe.wait_ge(s_["ht_ok"], n * NJ + j + 1)
                    for b in range(BG):
                        if width <= 256:
                            bank, c0 = 2 + b // 2, (b % 2) * width
                            if b % 2 == 0:
                                wait(pe, s_["proj_mv"], (n * NJ + j) * BG + b - 2)
                            ins = pe.matmul(ps[bank][:, c0:c0 + width], HT[0:k, q, b * P:(b + 1) * P], w[0:k, :], start=True, stop=True)
                        elif not has_nodes(j, b):
                            continue
                        else:
                            wait(pe, s_["proj_mv"], (n * NJ + j) * BG + b - 1)
                            for w0 in range(0, width, 512):
                                ins = pe.matmul(ps[2 + 2 * (b % 2) + w0 // 512][:], HT[0:k, q, b * P:(b + 1) * P], w[0:k, w0:w0 + 512],
                                                start=True, stop=True)
                        ins.then_inc(s_["proj_ps"], blocks_done(j, b) if width > 256 else 1)

                turn(0, 0)
                for j in (0, 1):
                    turn(j + 1, 1 - j)
                    products(j, j)
                with pe.Fori(1, (NJ - 1) // 2) as i:
                    for h in range(2):
                        turn(i * 2 + (h + 1), 1 - h)
                        products(i * 2 + h, h)
                products(NJ - 1, 0)

            def segment(n):
                def groups(i):
                    for r in range(R):
                        pe.wait_ge(gather_ok[r], i * (16 * G) + (n * (NG // R) + 1) * 16 * G)
                        pe.wait_ge(s_["S_ok"], i * R + n * NG + r + 1)
                        wait(pe, s_["acc_ok"], (i * R + n * NG + r - 1) * G)
                        for k in range(G):
                            ins = pe.matmul(ps[6 + r % 2][:, k * D:(k + 1) * D], S[:, r % 2, k, :], gat[:, r, k * D:(k + 1) * D],
                                            start=True, stop=True)
                        ins.then_inc(s_["mm_ok"], 1)

                turns(pe, NG // R, groups)

            pe.wait_ge(s_["mlp_c"], 3)
            pe.wait_ge(s_["w0_ok"], 1)
            project(0, W0, 2 * D, DA)
            pe.wait_ge(s_["proj_mv"], NJ * BG)

            def columns(c, h):
                pe.wait_ge(s_["stair_f"], c + 1)
                for f in range(4):
                    src_ap = fld[:, f * P:(f + 1) * P] if f != 2 else rec_buf[h][:, 2 * P:3 * P]
                    pe.transpose(ps[4][:, f * P:(f + 1) * P], src_ap, ident[:])
                wait(pe, s_["stair_e"], c)
                for a in range(EA):
                    ins = pe.transpose(ps[5 + a // 4][:, (a % 4) * P:(a % 4 + 1) * P],
                                       rec_buf[h][:, 4 * P:(4 + EA) * P].rearrange("p (e a) -> p a e", a=EA)[:, a, :], ident[:])
                ins.then_inc(s_["stair_T"], 1)

            column_turns(pe, columns)
            pe.wait_ge(s_["stair_e"], NC)
            pe.wait_ge(s_["stair_done"], 1)
            segment(0)
            pe.wait_ge(s_["rel_in"], 16)
            project(1, WR, NREL * D, D)
            segment(1)
            regs = [pe.alloc_register(f"pe_blk{k}") for k in range(G)]

            def spread(bank, g, h, attributes):
                pe.reg_load(regs, blkR[0:1, bass.ds(g * G, G)])
                cols = [pe.snap(x_, min_val=0, max_val=(NODE_BLOCKS - 1) * D) for x_ in regs]
                if attributes:
                    pe.matmul(ps[bank][:], attrT[:, h, :], Web[:].rearrange("p k f -> p (k f)"), start=True, stop=True)
                for k in range(G):
                    ins = pe.matmul(ps[bank][:, k * D:(k + 1) * D], ST[:, h, k, :], AG[:, bass.ds(cols[k], D)],
                                    start=not attributes, stop=True, skip_group_check=attributes)
                return ins

            for m in range(NH):
                def spread_next(g, h):
                    pe.wait_ge(s_["hop_ST"], m * NG + g + 1)
                    spread(h, g, h, False).then_inc(s_["msg_ps"], 1)

                def hops(i):
                    for r in range(R):
                        g, h = i * R + r, r % 2
                        if not (isinstance(g, int) and g == NG - 1):
                            spread_next(g + 1, 1 - h)
                        pe.wait_ge(s_["msg_ok"], m * NG + g + 1)
                        wait(pe, s_["rows_ok"], m * NG + g - 1)
                        for k in range(G):
                            ins = pe.matmul(ps[2 + h][:, k * D:(k + 1) * D], S[:, h, k, :], pre[:, h, k * D:(k + 1) * D],
                                            start=True, stop=True)
                        ins.then_inc(s_["sum_ps"], 1)

                spread_next(0, 0)
                turns(pe, NG // R, hops)
            project(2, W4, 4 * D, DA)
            pe.wait_ge(s_["web_in"], 16 * G)

            def attr_turn(g, i, r):
                pe.wait_ge(attr_in[r], (i + 1) * 16)
                if not isinstance(g, int):
                    pe.sem_inc(s_["turns_begun"], 1)
                pe.transpose(ps[5 * (r % 2)][0:G * EA, 0:P], attrG[:, r, :], ident[:]).then_inc(s_["aT_ps"], 1)

            def first_layer(g, h):
                pe.wait_ge(s_["ST_ok"], g + 1)
                pe.wait_ge(s_["aT_ok"], g + 1)
                spread(1, g, h, True).then_inc(s_["pre_ps"], 1)

            def third_layer(g):
                pe.wait_ge(s_["h2_ok"], g + 1)
                for k in range(G // 2):
                    ins = pe.matmul(ps[4][:, 2 * k:2 * k + 2], h2r[:, k * P:(k + 1) * P], W3t[:], start=True, stop=True)
                ins.then_inc(s_["e_ps"], 1)

            def segment_edges(g, r):
                h = r % 2
                pe.wait_ge(s_["ge_ok"], g + 1)
                pe.wait_ge(s_["acc_ok"], (EDGE * NG + g - 1) * G)
                for k in range(G):
                    ins = pe.matmul(ps[6 + h][:, k * D:(k + 1) * D], S[:, h, k, :], gat[:, r, k * 2 * D:k * 2 * D + D],
                                    start=True, stop=True)
                ins.then_inc(s_["mm_ok"], 1)

            def edges(i):
                for r in range(R):
                    g = i * R + r
                    last = isinstance(g, int) and g == NG - 1
                    if not (isinstance(g, int) and g >= NG - 2):
                        attr_turn(g + 2, i if r < R - 2 else i + 1, (r + 2) % R)
                    pe.wait_ge(s_["pre_ok"], g + 1)
                    for k in range(G // 2):
                        ins = pe.transpose(ps[2][:, k * P:(k + 1) * P], pre[:, 0, k * P:(k + 1) * P], ident[:])
                    ins.then_inc(s_["h1_ps"], 1)
                    if not (isinstance(g, int) and g == 0):
                        third_layer(g - 1)
                    if not last:
                        first_layer(g + 1, (r + 1) % 2)
                    pe.wait_ge(s_["h1_ok"], g + 1)
                    pe.matmul(ps[3][0:2 * H2, :], W2t[:], h1r[:], start=True, stop=True).then_inc(s_["h2_ps"], 1)
                    if not (isinstance(g, int) and g == 0):
                        segment_edges(g - 1, (r - 1) % R)

            attr_turn(0, 0, 0)
            attr_turn(1, 0, 1)
            first_layer(0, 0)
            turns(pe, NG // R, edges)
            third_layer(NG - 1)
            segment_edges(NG - 1, R - 1)

        @block.vector
        def _(dve):
            steps = [0]

            def chain(ins):
                steps[0] += 1
                ins.then_inc(s_["dve"], 1)
                dve.wait_ge(s_["dve"], steps[0])

            dve.memset(X[:], 0.0)
            dve.memset(dstI, PAD_DST)
            dve.memset(srcI, 0)
            dve.memset(wI, 0)
            chain(dve.memset(tyI, 0))
            dve.sem_inc(s_["zero_ok"], 1)
            dve.memset(pre[:], 0.0)
            dve.memset(W2n[:], 0.0)
            dve.memset(W3n[:], 0.0)
            dve.memset(Web[:], 0.0)
            chain(dve.memset(H[:], 1.0))
            dve.sem_inc(s_["zero_ok"], 1)
            dve.wait_ge(s_["pool_const"], 7)
            dve.tensor_copy(iotaN[:], iotaI[:])
            chain(dve.tensor_copy(iotaP[:], iotaPi[:]))
            dve.tensor_scalar(junkP[:], iotaP[:], float(NP), None, ALU.add)
            chain(dve.tensor_copy(stepN[:], tile_i[:]))
            dve.sem_inc(s_["const_ok"], 1)
            dve.wait_ge(s_["edges_in"], 16 * 8)
            hi = TMP[:, 0:STEPS].bitcast(I32)
            dve.tensor_scalar(hi, srcI, 7, None, ALU.logical_shift_right)
            chain(dve.tensor_scalar(srcI, srcI, P - 1, None, ALU.bitwise_and))
            chain(dve.scalar_tensor_tensor(srcI, srcI, float(NB), hi, ALU.mult, ALU.add))
            dve.sem_inc(s_["src_rows"], 1)
            dv = dstI.rearrange("p (c j) -> p c j", j=P)
            dve.tensor_scalar(edgeB[:, 0, :], dv[:, :, 0], 7, None, ALU.logical_shift_right)
            chain(dve.tensor_scalar(edgeB[:, 1, :], dv[:, :, P - 1], 7, None, ALU.logical_shift_right))
            chain(dve.tensor_copy(blo[:], edgeB[:, 0, :]))
            chain(dve.tensor_copy(cnt[:], edgeB[:, 1, :]))
            chain(dve.scalar_tensor_tensor(cnt[:], cnt[:], 1.0, blo[:], ALU.add, ALU.subtract))
            chain(dve.tensor_reduce(tot[:], cnt[:], AX.X, ALU.add))
            dve.sem_inc(s_["base_mm"], 1)
            dve.wait_ge(s_["base_mm"], 2)
            chain(dve.tensor_copy(start[:, 0:1], ps[7][:, 0:1]))
            for c in range(1, NC):
                chain(dve.tensor_tensor(start[:, c:c + 1], start[:, c - 1:c], cnt[:, c - 1:c], ALU.add))
            chain(dve.tensor_tensor(q[:], blo[:], start[:], ALU.subtract))
            dve.sem_inc(s_["tiles_ok"], 1)
            parts = [0]

            def layernorm(blk0, blk1):
                parts[0] += 1
                xb, hb, tb = Xv[:, blk0:blk1], Hv[:, blk0:blk1], TMPv[:, blk0:blk1]
                t1, t2, t3 = s1[:, blk0:blk1], s2[:, blk0:blk1], s3[:, blk0:blk1]
                per_row = t1.rearrange("p (b u) -> p b u", u=1).to_broadcast([P, blk1 - blk0, D])
                chain(dve.tensor_reduce(t1, xb, AX.X, ALU.add))
                chain(dve.tensor_scalar(t1, t1, 1.0 / D, None, ALU.mult))
                chain(dve.tensor_tensor(hb, xb, per_row, ALU.subtract))
                chain(dve.tensor_tensor(tb, hb, hb, ALU.mult))
                chain(dve.tensor_reduce(t2, tb, AX.X, ALU.add))
                chain(dve.tensor_scalar(t2, t2, 1.0 / D, LN_EPS, ALU.mult, ALU.add))
                dve.sem_inc(s_["ln_var"], 1)
                dve.wait_ge(s_["ln_std"], parts[0])
                chain(dve.reciprocal(t1, t3))
                chain(dve.scalar_tensor_tensor(hb, hb, 0.0, per_row, ALU.max, ALU.mult))
                dve.sem_inc(s_["ln_ok"], 1)

            dve.wait_ge(s_["x_in"], 32)
            layernorm(0, LN_SPLIT)
            dve.wait_ge(s_["w_in"], 16 * 5)
            for half, wv in enumerate((srcT, rowT)):
                v = wv[0:DA, 0:D * NBASE].bitcast(F32).rearrange("i (o b) -> i o b", b=NBASE)
                c3 = linB[:].rearrange("i (u b) -> i u b", u=1).to_broadcast([DA, D, NBASE])
                chain(dve.tensor_tensor(v, v, c3, ALU.mult))
                chain(dve.tensor_reduce(W0[:, half * D:(half + 1) * D], v, AX.X, ALU.add))
            dve.sem_inc(s_["w0_ok"], 1)
            layernorm(LN_SPLIT, NB)
            dve.wait_ge(s_["start_in"], 16)
            first = [max(0, c * P - (NODE_BLOCKS - 1)) for c in range(NC)]
            wide_c = P + NODE_BLOCKS - 1
            begun = [TMP[:, c * wide_c:c * wide_c + (c + 1) * P - first[c]] for c in range(NC)]
            for c in range(NC):
                last = dve.tensor_scalar(begun[c], startB[:, first[c]:(c + 1) * P], stepN[:, c:c + 1], None, ALU.is_le)
            chain(last)
            for c in range(NC):
                last = dve.tensor_reduce(cnt[:, c:c + 1], begun[c], AX.X, ALU.add)
            chain(last)
            for c in range(NC):
                last = dve.tensor_scalar(tile_i[:, c:c + 1], cnt[:, c:c + 1], float(first[c] - 1), None, ALU.add)
            chain(last)

            def tiles_of(c, h):
                dve.tensor_copy(tcol[:, h:h + 1], tile_i[:, bass.ds(c, 1)]).then_inc(s_["tcol_ok"], 1)

            def columns(c, h):
                rec = rec_buf[h][:].bitcast(I32)
                dve.wait_ge(stair_g[h], (c + 2 - h) * 8)
                wait(dve, s_["stair_out"], c * 48)
                dve.tensor_tensor(blkf[:], rec_buf[h][:, RW - 1:RW], stepN[:, bass.ds(c, 1)], ALU.add)
                dve.tensor_copy(fld[:, 0:P], rec[:, 0:P])
                dve.tensor_copy(fld16[:, 0, :], rec[:, 0:P])
                dve.tensor_copy(fld[:, P:2 * P], rec[:, P:2 * P])
                dve.tensor_copy(fld[:, 3 * P:4 * P], rec[:, 3 * P:4 * P]).then_inc(s_["stair_d"], 1)
                dve.wait_ge(s_["stair_d"], c * 3 + 1)
                dve.tensor_scalar(blki[:], blkf[:], float(D), None, ALU.mult)
                dve.tensor_scalar(nblk[:], blkf[:], -float(P), None, ALU.mult)
                dve.scalar_tensor_tensor(fld[:, 3 * P:4 * P], fld[:, 0:P], float(NREL), fld[:, 3 * P:4 * P],
                                         ALU.mult, ALU.add).then_inc(s_["stair_d"], 1)
                dve.wait_ge(s_["stair_d"], c * 3 + 2)
                dve.tensor_scalar(fld16[:, 1, :], fld[:, P:2 * P], nblk[:, 0:1], None, ALU.add)
                dve.tensor_scalar(fld[:, P:2 * P], fld[:, P:2 * P], nblk[:, 0:1], None, ALU.add).then_inc(s_["stair_f"], 1)
                dve.wait_ge(s_["stair_T"], c + 1)
                if not (isinstance(c, int) and c >= NC - 2):
                    tiles_of(c + 2, h)
                dve.tensor_copy(srcT[:, bass.ds(c * P, P)], ps[4][:, 0:P])
                dve.tensor_copy(relT[:, bass.ds(c * P, P)], ps[4][:, P:2 * P])
                dve.tensor_copy(wT[:, bass.ds(c * P, P)], ps[4][:, 2 * P:3 * P])
                dve.tensor_copy(rowT[:, bass.ds(c * P, P)], ps[4][:, 3 * P:4 * P]).then_inc(s_["stair_d"], 1)
                dve.wait_ge(s_["stair_d"], c * 3 + 3)

            tiles_of(0, 0)
            tiles_of(1, 1)
            column_turns(dve, columns)
            dve.sem_inc(s_["stair_done"], 1)
            def steps_of(t, g, width=P):
                return t[:, bass.ds(g * G, G)].rearrange("p (k u) -> p k u", u=1).to_broadcast([P, G, width])

            def steps_of1(t):
                return t[:].rearrange("p (k u) -> p k u", u=1).to_broadcast([P, G, D])

            nview = iotaN[:].rearrange("p (u n) -> p u n", u=1).to_broadcast([P, G, P])

            def one_hot(n, g, h):
                wait(dve, s_["mm_ok"], n * NG + g + (R - 1))
                dve.tensor_tensor(S[:, h, :, :], steps_of(relT, g), nview, ALU.is_equal).then_inc(s_["S_ok"], 1)

            regs = [dve.alloc_register(f"dve_blk{k}") for k in range(G)]

            def accumulate(n, i, r, acc):
                dve.reg_load(regs, blkR[0:1, bass.ds(i * (R * G) + r * G, G)])
                cols = [dve.snap(x_, min_val=0, max_val=(NODE_BLOCKS - 1) * D) for x_ in regs]
                dve.wait_ge(s_["mm_ok"], i * R + (n * NG + r + R + 1))
                for k in range(G):
                    if not (isinstance(i, int) and n == 0 and (i * R + r) * G + k < 2):
                        dve.wait_ge(s_["acc_ok"], i * (R * G) + ((n * NG + r) * G + k - 1))
                    a = (acc, TMP)[k % 2][:, bass.ds(cols[k], D)]
                    dve.tensor_tensor(a, a, ps[6 + r % 2][:, k * D:(k + 1) * D], ALU.add).then_inc(s_["acc_ok"], 1)

            def message_pass(n, acc):
                chain(dve.memset(TMP[:], 0.0))
                one_hot(n, 0, 0)

                def groups(i):
                    for r in range(R):
                        g = i * R + r
                        if not (isinstance(g, int) and g == NG - 1):
                            one_hot(n, g + 1, (r + 1) % 2)
                        accumulate(n, i, r, acc)

                turns(dve, NG // R, groups)
                dve.wait_ge(s_["acc_ok"], (n + 1) * NG * G)

            dve.wait_ge(s_["blk_in"], 16)
            message_pass(0, AG)
            for part, (blk0, blk1) in enumerate(((0, LN_SPLIT), (LN_SPLIT, NB))):
                xb, ab, tb = Xv[:, blk0:blk1], AGv[:, blk0:blk1], TMPv[:, blk0:blk1]
                t1, t2, t3 = s1[:, blk0:blk1], s2[:, blk0:blk1], s3[:, blk0:blk1]
                per_row = t1.rearrange("p (b u) -> p b u", u=1).to_broadcast([P, blk1 - blk0, D])
                chain(dve.tensor_tensor(ab, ab, tb, ALU.add))
                chain(dve.tensor_tensor(tb, ab, ab, ALU.mult))
                chain(dve.tensor_reduce(t2, tb, AX.X, ALU.add))
                dve.sem_inc(s_["nrm_in"], 1)
                dve.wait_ge(s_["nrm_out"], part + 1)
                chain(dve.tensor_scalar(t1, t3, L2_EPS, None, ALU.max))
                chain(dve.reciprocal(t1, t1))
                chain(dve.tensor_tensor(ab, ab, per_row, ALU.mult))
                chain(dve.tensor_tensor(xb, xb, ab, ALU.add))
                layernorm(blk0, blk1)
            message_pass(1, X)
            chain(dve.tensor_tensor(X[:], X[:], TMP[:], ALU.add))
            layernorm(0, NB)
            dve.wait_ge(s_["tabs_zero"], 16 * NH * NT)
            chain(dve.tensor_copy(AGv, Hv))
            mask = lower[:].rearrange("p (u n) -> p u n", u=1).to_broadcast([P, G, P])
            for m in range(NH):

                def spreader(g, i, r):
                    dve.wait_ge(rows_in[r], (m * (NG // R) + i + 1) * 32)
                    dve.tensor_scalar(ST[:, r % 2, :, :].rearrange("p k e -> p (k e)"), raw[:, r, 0, :], iotaP[:, 0:1], None,
                                      ALU.is_equal).then_inc(s_["hop_ST"], 1)

                def same_src(g, r):
                    wait(dve, s_["sum_ps"], m * NG + g - 1)
                    dve.tensor_tensor(S[:, r % 2, :, :], raw[:, r, 1, :].rearrange("p (k e) -> p k e", k=G), steps_of(srcT, g),
                                      ALU.is_equal).then_inc(s_["hop_M"], 1)

                def targets(g, h):
                    dve.wait_ge(s_["hop_M"], g + 1)
                    wait(dve, s_["dup_ok"], g * 4)
                    later = TMP[:, 0:G * P].rearrange("p (k e) -> p k e", k=G)
                    dve.tensor_tensor(later, S[:, h, :, :], mask, ALU.mult).then_inc(s_["dup_ok"], 1)
                    dve.tensor_scalar(away[:], srcT[:, bass.ds(g * G, G)], -1.0, junkP[:, 0:1], ALU.mult, ALU.add)
                    dve.wait_ge(s_["dup_ok"], g * 4 + 1)
                    dve.tensor_reduce(dups[:], later, AX.X, ALU.add).then_inc(s_["dup_ok"], 1)
                    dve.wait_ge(s_["dup_ok"], g * 4 + 2)
                    dve.scalar_tensor_tensor(away[:], dups[:], 0.5, away[:], ALU.is_gt, ALU.mult).then_inc(s_["dup_ok"], 1)
                    dve.wait_ge(s_["dup_ok"], g * 4 + 3)
                    dve.tensor_tensor(rowT[:, bass.ds(g * G, G)], away[:], srcT[:, bass.ds(g * G, G)], ALU.add).then_inc(s_["dup_ok"], 1)

                def weighted(g, r):
                    dve.wait_ge(s_["msg_ps"], m * NG + g + 1)
                    dve.tensor_tensor(pre[:, r % 2, :].rearrange("p (k f) -> p k f", f=D),
                                      ps[r % 2][:].rearrange("p (k f) -> p k f", f=D),
                                      steps_of(wT, g, D), ALU.mult).then_inc(s_["msg_ok"], 1)

                def ahead(g, r):
                    same_src(g, r)
                    if m == 0:
                        targets(g, r % 2)
                    weighted(g, r)

                def groups(i):
                    for r in range(R):
                        g = i * R + r
                        if not (isinstance(g, int) and g == NG - 1):
                            ahead(g + 1, (r + 1) % R)
                        if not (isinstance(g, int) and g >= NG - 2):
                            spreader(g + 2, i if r < R - 2 else i + 1, (r + 2) % R)

                spreader(0, 0, 0)
                ahead(0, 0)
                spreader(1, 0, 1)
                if m > 0:
                    chain(dve.tensor_tensor(Hv, Hv, AGv, ALU.add))
                if m == NH - 1:
                    chain(dve.scalar_tensor_tensor(Xv, Hv, 0.25, Xv, ALU.mult, ALU.add))
                turns(dve, NG // R, groups)
                dve.wait_ge(s_["sum_ps"], (m + 1) * NG)
                dve.sem_inc(s_["hop_done"], 1)
                for half in range(2):
                    dve.wait_ge(sum_in[0][half], (m + 1) * 16)
                for t in range(1, NT):
                    loads, so_far = (NT // 2, (t + 1) // 2) if t % 2 else (NT // 2 - 1, t // 2)
                    for half in range(2):
                        dve.wait_ge(sum_in[sum_sem(t)][half], (m * loads + so_far) * 16)
                        cols = slice(half * NB // 2 * D, (half + 1) * NB // 2 * D)
                        chain(dve.tensor_tensor(AG[:, cols], AG[:, cols], sum_buf(t)[:, cols], ALU.add))
                        dve.sem_inc(s_["sum_mv"], 1)
            for blk0, blk1 in ((0, LN_SPLIT), (LN_SPLIT, NB)):
                chain(dve.scalar_tensor_tensor(Xv[:, blk0:blk1], AGv[:, blk0:blk1], 0.25, Xv[:, blk0:blk1], ALU.mult, ALU.add))
                layernorm(blk0, blk1)

            def spreader(g, i, r):
                dve.wait_ge(rows_in[r], NH * (NG // R) * 32 + (i + 1) * 16)
                dve.tensor_scalar(ST[:, r % 2, :, :].rearrange("p k e -> p (k e)"), raw[:, r, 0, :], iotaP[:, 0:1], None,
                                  ALU.is_equal).then_inc(s_["ST_ok"], 1)

            def rows_of(r, part):
                return gat[:, r, :].rearrange("p (k f) -> p k f", f=2 * D)[:, :, part * D:(part + 1) * D]

            def first_layer(g, i, r):
                dve.wait_ge(s_["pre_ps"], g + 1)
                dve.wait_ge(gather_ok[r], i * (16 * G) + (EDGE * (NG // R) + 1) * 16 * G)
                dve.tensor_tensor(pre[:, 0, :].rearrange("p (k f) -> p k f", f=D), ps[1][:].rearrange("p (k f) -> p k f", f=D),
                                  rows_of(r, 1), ALU.add).then_inc(s_["pre_ok"], 1)

            def scale(g, r):
                dve.wait_ge(s_["e_ps"], g + 1)
                dve.tensor_scalar(esc[:], ps[4][:, 0:G], b3c[:, 0:1], 0.0, ALU.add, ALU.max).then_inc(s_["esc_ok"], 1)
                dve.wait_ge(s_["esc_ok"], g + 1)
                dve.tensor_tensor(rows_of(r, 0), rows_of(r, 0), steps_of1(esc), ALU.mult).then_inc(s_["ge_ok"], 1)

            def edges(i):
                for r in range(R):
                    g = i * R + r
                    if not (isinstance(g, int) and g < 2):
                        accumulate(EDGE, i if r >= 2 else i - 1, (r + 2) % R, X)
                    dve.wait_ge(s_["h1_sb"], g + 1)
                    dve.scalar_tensor_tensor(h1r[:], h1[:], NEG_SLOPE, h1[:], ALU.mult, ALU.max).then_inc(s_["h1_ok"], 1)
                    if not (isinstance(g, int) and g == 0):
                        scale(g - 1, (r - 1) % R)
                    one_hot(EDGE, g, r % 2)
                    if not (isinstance(g, int) and g >= NG - 2):
                        spreader(g + 2, i if r < R - 2 else i + 1, (r + 2) % R)
                    dve.wait_ge(s_["h2_sb"], g + 1)
                    dve.scalar_tensor_tensor(h2r[:], h2[:], NEG_SLOPE, h2[:], ALU.mult, ALU.max).then_inc(s_["h2_ok"], 1)
                    if not (isinstance(g, int) and g == NG - 1):
                        first_layer(g + 1, i if r < R - 1 else i + 1, (r + 1) % R)

            spreader(0, 0, 0)
            first_layer(0, 0, 0)
            spreader(1, 0, 1)
            turns(dve, NG // R, edges)
            scale(NG - 1, R - 1)
            for r in (R - 2, R - 1):
                accumulate(EDGE, NG // R - 1, r, X)
            dve.wait_ge(s_["acc_ok"], (EDGE + 1) * NG * G)
            chain(dve.tensor_tensor(X[:], X[:], TMP[:], ALU.add))
            dve.sem_inc(s_["pass_ok"], 1)


_INS = ['x', 'src', 'dst', 'edge_attr_8', 'edge_type_16', 'edge_weight', 'L0_gnn_basis_msg_wt', 'L0_gnn_basis_msg_bias',
        'L0_gnn_basis_self_wt', 'L0_gnn_basis_self_bias', 'L0_gnn_lin_comb', 'L1_gnn_weight', 'L3_gnn_W_src', 'L3_gnn_b_src',
        'L3_gnn_W_tgt', 'L3_gnn_b_tgt', 'L3_gnn_W_edge', 'L3_gnn_b_edge', 'L3_gnn_W1', 'L3_gnn_b1', 'L3_gnn_W2', 'L3_gnn_b2',
        'L3_gnn_W3', 'L3_gnn_b3']


def kernel(**inputs):
    import numpy as _np
    import concourse.bacc as _bacc
    from concourse import mybir as _mybir
    from concourse.bass_utils import run_bass_kernel_spmd as _run

    nc = _bacc.Bacc("TRN2", target_bir_lowering=False, num_devices=1)
    arrays, args = {}, []
    for name in _INS:
        a = _np.ascontiguousarray(inputs[name])
        arrays[f"in_{name}_dram"] = a
        args.append(nc.dram_tensor(f"in_{name}_dram", a.shape, _mybir.dt.from_np(a.dtype), kind="ExternalInput").ap())
    o = nc.dram_tensor("out_0_dram", inputs['x'].shape, _mybir.dt.float32, kind="ExternalOutput").ap()
    gnn_kernel(nc, *args, o)
    r = _run(nc, [arrays], core_ids=[0])
    return r.results[0]["out_0_dram"]
```
